# Optimizing a Trainium2 kernel written in Bass

```python
import numpy as np
import jax
import jax.numpy as jnp

def _softmax(x, axis=-1):
    return jax.nn.softmax(x, axis=axis)
def _gelu(x):
    return jax.nn.gelu(x, approximate=True)
def _silu(x):
    return jax.nn.silu(x)
def _sigmoid(x):
    return jax.nn.sigmoid(x)
def _layernorm(x, axis=-1, eps=1e-5):
    m = jnp.mean(x, axis=axis, keepdims=True)
    v = jnp.var(x, axis=axis, keepdims=True)
    return (x - m) / jnp.sqrt(v + eps)
def _scatter_add(tgt, idx, src, axis=0):
    return tgt.at[idx].add(src)
def _segment_sum(src, seg, n):
    return jax.ops.segment_sum(src, seg, n)

kernel_name = 'mk_conv_preact_d2_conv_nchw32_65d742'

def setup_inputs(seed: int = 0):
    np.random.seed(seed)
    _w = jnp.asarray
    def _rec_inputs():
        import jax
        import jax.numpy as jnp
        _gk = jax.random.key(seed)
        x = -7.109e-05 + 0.9999 * jax.random.normal(jax.random.fold_in(_gk, 1), (8, 32, 512, 512), jnp.float32)
        return x
    x = _rec_inputs()
    def _L0_conv_setup():
        import jax, jax.numpy as jnp
        import numpy as np
        key = jax.random.key(seed)
        k1, k2, k3, k4 = jax.random.split(key, 4)
        B, Cin, Cout, R = (8, 32, 32, 32)
        H, W = (512, 512)
        M1, M2 = (32, 32)
        return {'x': jax.random.normal(k1, (B, Cin, H, W), dtype=jnp.float32), 'coeff_real': jax.random.normal(k2, (R, M1, M2, Cin), dtype=jnp.float32), 'coeff_imag': jax.random.normal(k3, (R, M1, M2, Cin), dtype=jnp.float32), 'proj': jax.random.normal(k4, (Cout, R), dtype=jnp.float32)}
    _L0_conv_all = _L0_conv_setup()
    _L0_conv_in = {k: v for k, v in _L0_conv_all.items() if k in ('coeff_real', 'coeff_imag', 'proj', )}
    del _L0_conv_all

    def _L1_conv_setup():
        import jax, jax.numpy as jnp
        import numpy as np
        key = jax.random.key(seed)
        k1, k2 = jax.random.split(key)
        x = jax.random.normal(k1, (8, 32, 252, 252), dtype=jnp.float32)
        weight = jax.random.normal(k2, (32, 32, 5, 5), dtype=jnp.float32)
        return {'x': x, 'weight': weight}
    _L1_conv_all = _L1_conv_setup()
    _L1_conv_in = {k: v for k, v in _L1_conv_all.items() if k in ('weight', )}
    del _L1_conv_all

    return {
        "x": x,
        "L0_conv_coeff_real": _L0_conv_in["coeff_real"],
        "L0_conv_coeff_imag": _L0_conv_in["coeff_imag"],
        "L0_conv_proj": _L0_conv_in["proj"],
        "L1_conv_weight": _L1_conv_in["weight"],
    }

def reference(x, L0_conv_coeff_real, L0_conv_coeff_imag, L0_conv_proj, L1_conv_weight):
    import jax
    import jax.numpy as jnp
    def _L0_conv_ref(x, coeff_real, coeff_imag, proj):
        import jax, jax.numpy as jnp
        import numpy as np
        M1, M2 = (coeff_real.shape[1], coeff_real.shape[2])
        B, Cin, H, W = x.shape
        Cout = proj.shape[0]
        Wc = jnp.einsum('or,rijc->oijc', proj, coeff_real) + 1j * jnp.einsum('or,rijc->oijc', proj, coeff_imag)
        x_ft = jnp.fft.rfftn(x, axes=(-2, -1))
        m1 = min(M1, x_ft.shape[-2])
        m2 = min(M2, x_ft.shape[-1])
        out_modes = jnp.einsum('bcij,oijc->boij', x_ft[:, :, :m1, :m2], Wc[:, :m1, :m2, :])
        out_ft = jnp.zeros((B, Cout, H, x_ft.shape[-1]), dtype=x_ft.dtype)
        out_ft = out_ft.at[:, :, :m1, :m2].set(out_modes)
        return jnp.fft.irfftn(out_ft, s=(H, W), axes=(-2, -1))

    def _L1_conv_ref(x, weight):
        import jax, jax.numpy as jnp
        import numpy as np
        k = weight.shape[-1]
        p = k // 2
        xp = jnp.pad(x, ((0, 0), (0, 0), (p, p), (p, p)), mode='reflect')
        H, W = (xp.shape[-2], xp.shape[-1])
        wp = jnp.zeros((weight.shape[0], weight.shape[1], H, W), dtype=x.dtype)
        wp = wp.at[:, :, :k, :k].set(weight)
        shift = -k // 2
        wp = jnp.roll(wp, shift=(shift, shift), axis=(-2, -1))
        x_fft = jnp.fft.fft2(xp)
        w_fft = jnp.fft.fft2(wp)
        out_fft = jnp.einsum('bihw,oihw->bohw', x_fft, w_fft)
        out = jnp.fft.ifft2(out_fft).real
        return out[:, :, p:-p, p:-p]

    def _gn(v, G=16, eps=1e-5):
        B_, C_, H_, W_ = v.shape
        g = v.reshape(B_, G, C_ // G, H_, W_)
        m = jnp.mean(g, axis=(2, 3, 4), keepdims=True)
        s = jnp.var(g, axis=(2, 3, 4), keepdims=True)
        return ((g - m) / jnp.sqrt(s + eps)).reshape(v.shape)

    def _ln_c(v, eps=1e-6):
        m = jnp.mean(v, axis=1, keepdims=True)
        s = jnp.var(v, axis=1, keepdims=True)
        return (v - m) / jnp.sqrt(s + eps)

    def _ln_t(v, eps=1e-5):
        m = jnp.mean(v, axis=-1, keepdims=True)
        s = jnp.var(v, axis=-1, keepdims=True)
        return (v - m) / jnp.sqrt(s + eps)

    def _to_tokens(v):
        B_, C_, H_, W_ = v.shape
        return v.reshape(B_, C_, H_ * W_).transpose(0, 2, 1)
    def _from_tokens(t, like):
        B_, C_, H_, W_ = like.shape
        return t.transpose(0, 2, 1).reshape(B_, C_, H_, W_)

    x = x + _L0_conv_ref(_gn(x), L0_conv_coeff_real, L0_conv_coeff_imag, L0_conv_proj)
    x = x + _L1_conv_ref(_gn(x), L1_conv_weight)
    return x


_drawn_inputs = setup_inputs


def setup_inputs(seed=0):
    import zlib

    import numpy as np

    out = dict(_drawn_inputs(seed))
    spreads = {}
    factors = {}
    for name, (base, spread) in spreads.items():
        noise = np.random.default_rng([zlib.crc32(name.encode()), seed]).standard_normal(out[name].shape)
        drawn = base * np.exp(spread * noise) if base else spread * noise
        out[name] = jnp.asarray(drawn.astype(out[name].dtype))
    for name, factor in factors.items():
        out[name] = (out[name] * factor).astype(out[name].dtype)
    return out
```

```python
from contextlib import ExitStack

import numpy as np
import concourse.bass as bass
from concourse import mybir

F32 = mybir.dt.float32
F16 = mybir.dt.float16
ALU = mybir.AluOpType
ACT = mybir.ActivationFunctionType
AX = mybir.AxisListType

P = 128
C = 32
M1 = 32
M2 = 32
KB = P // C
KI = M1 // KB
TAPS = 5
SLOTS = 4
RING = 4
G_SCALE = 64.0
W_SCALE = 1024.0
Y_SCALE = 16384.0
GN_EPS = 1e-5
TINY = 1e-30

IDENT, MEAN, PAIR, PAIR_ALL, DC_DEV, DC_PAIR, CHAN = range(7)
ALPHA, GAIN, SHIFT = range(3)


def constant_tables(H, W):
    f = np.float64
    k1 = np.arange(M1).reshape(KB, KI)
    h = np.arange(H).reshape(P, H // P)
    ang = 2 * np.pi * h[:, :, None, None] * k1.T[None, None] / H
    dft_h = np.stack([np.cos(ang), -np.sin(ang)], axis=3).reshape(P, H // P, 2 * M1)
    w = np.arange(W).reshape(W // P, P).T
    ang = 2 * np.pi * w[:, :, None] * np.arange(M2) / W
    c, s = np.cos(ang), np.sin(ang)
    dft_w = np.stack([np.concatenate([c, -s], -1), np.concatenate([s, c], -1)], axis=2)
    Q = H // KB
    rows = np.empty((Q + 1, KB), int)
    rows[:Q, :3] = KB * np.arange(Q)[:, None] + np.arange(3)
    rows[1:, 3] = KB * np.arange(1, Q + 1) - 1
    rows[0, 3] = 1
    rows[Q, :3] = H - 2, H - 3, 2
    ang = 2 * np.pi * k1.reshape(-1, 1) * rows.reshape(1, -1) / H
    idft_h = np.zeros((M1, 4, rows.size))
    idft_h[:, 0], idft_h[:, 1] = np.cos(ang), np.sin(ang)
    ang = 2 * np.pi * np.arange(M2)[:, None] * np.arange(W)[None] / W
    fold = np.where(np.arange(M2) == 0, 1.0, 2.0)[:, None]
    half = np.stack([fold * np.cos(ang), -fold * np.sin(ang)], axis=1).reshape(2 * M2, W)
    idft_w = np.concatenate([half, half])
    k = np.arange(P)[:, None]
    m = np.arange(P)[None]
    same_pair = (k % C) // 2 == (m % C) // 2
    mats = np.zeros((7, P, P))
    mats[IDENT] = k == m
    mats[MEAN] = 1.0 / P
    mats[PAIR] = 0.5 * (k // 2 == m // 2)
    mats[PAIR_ALL] = same_pair / (2.0 * (H * W) ** 2)
    mats[DC_PAIR] = (k < C) * same_pair * 0.5 / (H * W)
    mats[DC_DEV] = (k < C) * (k == m % C) / (H * W) - mats[DC_PAIR]
    mats[CHAN] = k % C == m % C
    cross = np.full((P, KI, 2, M2), 2.0)
    cross[..., 0] = 1.0
    own = np.full((P, KI, 2, M2), 2.0)
    own[..., 0] = 0.5
    for a in (cross, own):
        a[:C, 0, :, 0] = 0.0
    mode_weights = np.stack([cross, own], axis=1).reshape(P, 2, KI * 2 * M2)
    out = dict(dft_h=dft_h, dft_w=dft_w.reshape(P, W // P, 2, 2 * M2), idft_h=idft_h.reshape(P, -1),
               idft_w=idft_w, mats=mats.transpose(1, 0, 2), mode_weights=mode_weights)
    return {n: np.ascontiguousarray(a, dtype=np.float32) for n, a in out.items()}


def two_conv_layers(nc, x, coeff_re, coeff_im, proj, weight, dft_h, dft_w, idft_h, idft_w, mats,
                    mode_weights, out):
    B, _, H, W = x.shape
    HW = H * W
    HB, WB = H // P, W // P
    Q = H // KB
    NCH = Q // SLOTS
    GPS = C // 2
    MODES = KI * 2 * M2
    ds = bass.ds
    assert B % 2 == 0 and NCH % RING == 0

    top = ExitStack()
    with top:
        def sem(name):
            return top.enter_context(nc.semaphore(name))

        def keep(name, shape, dt=F32):
            return top.enter_context(nc.sbuf_tensor(name, shape, dt))

        modes_y = keep("modes_y", [P, B, MODES])
        scalars = keep("scalars", [P, B, 4])
        unscale = keep("unscale", [P, 1])
        taps = keep("taps", [P, 2, 2, TAPS, P], F16)
        rows_basis = keep("rows_basis", [P, (Q + 1) * KB])
        cols_hi = keep("cols_hi", [P, W], F16)
        cols_lo = keep("cols_lo", [P, W], F16)

        before_c = top.enter_context(ExitStack())

        def until_c(name, shape, dt=F32):
            return before_c.enter_context(nc.sbuf_tensor(name, shape, dt))

        modes_x = until_c("modes_x", [P, B, MODES])
        chan_stats = until_c("chan_stats", [P, B, C, 2])
        mat = until_c("mat", [P, 7, P])

        pa = ExitStack()
        with pa:
            def sb(name, shape, dt=F32):
                return pa.enter_context(nc.sbuf_tensor(name, shape, dt))

            LOADS = 4
            PAIRS = 2 * GPS
            x_pair = sb("x_pair", [P, LOADS, 2, HB * W])
            basis_h = sb("basis_h", [P, HB, 2 * M1])
            basis_w = sb("basis_w", [P, WB, 2, 2 * M2])
            z = sb("z", [P, 2, W])
            zt = sb("zt", [P, 2, WB, 2 * M1, C])
            bn = sb("bn", [P, 2, 2, HB, 6])
            two_stats = sb("two_stats", [P, 2, C, 2])
            z_ps = [pa.enter_context(nc.psum_tensor(f"z_ps{i}", [P, W], F32)) for i in range(2)]
            t_ps = [pa.enter_context(nc.psum_tensor(f"t_ps{i}", [P, WB, P], F32)) for i in range(2)]
            m_ps = [pa.enter_context(nc.psum_tensor(f"m_ps{i}", [P, MODES], F32)) for i in range(2)]

            const_in = sem("const_in")
            x_in = [sem(f"x_in{i}") for i in range(LOADS)]
            z_done, z_copied = sem("z_done"), sem("z_copied")
            t_done, t_copied = sem("t_done"), sem("t_copied")
            m_done = sem("m_done")
            agg_begun = sem("agg_begun")
            bn_done, bn_agg, stats_kept = sem("bn_done"), sem("bn_agg"), sem("stats_kept")

            xa = x.rearrange("b (g i) (p j) w -> b g p i (j w)", i=2, j=HB)
            NCONST = 3 * 16

            with nc.Block() as block:
                @block.sync
                def _(sp):
                    sp.dma_start(basis_h[:], dft_h).then_inc(const_in, 16)
                    sp.dma_start(basis_w[:], dft_w).then_inc(const_in, 16)
                    sp.dma_start(mat[:], mats).then_inc(const_in, 16)
                    for n in range(LOADS):
                        sp.dma_start(x_pair[:, n], xa[0, n]).then_inc(x_in[n], 16)

                    def refill(i, count):
                        for u in range(count):
                            sp.wait_ge(z_done, i * PAIRS + u + 1)
                            sp.wait_ge(bn_done, i * PAIRS + u + 1)
                            v = u + LOADS
                            sp.dma_start(x_pair[:, u % LOADS],
                                         xa[i * 2 + v // GPS, v % GPS]).then_inc(x_in[u % LOADS], 16)

                    if B > 2:
                        with sp.Fori(0, B // 2 - 1) as i:
                            refill(i, PAIRS)
                    refill(B // 2 - 1, PAIRS - LOADS)

                @block.tensor
                def _(pe):
                    pe.wait_ge(const_in, NCONST)

                    def row_modes(i, u):
                        pe.wait_ge(x_in[u % LOADS], i * (16 * PAIRS // LOADS) + 16 * (u // LOADS + 1))
                        for ch in range(2):
                            for j in range(HB):
                                last = nc.tensor.matmul(
                                    z_ps[u % 2][64 * ch:64 * ch + 64], basis_h[:, j],
                                    x_pair[:, u % LOADS, ch, j * W:(j + 1) * W],
                                    start=(j == 0), stop=(j == HB - 1))
                        last.then_inc(z_done, 1)

                    def transpose(i, u):
                        pe.wait_ge(z_copied, i * PAIRS + u + 1)
                        if u >= 2:
                            pe.wait_ge(t_copied, i * PAIRS + u - 1)
                        for k in range(WB):
                            last = nc.tensor.transpose(t_ps[u % 2][:, k], z[:, u % 2, k * P:(k + 1) * P],
                                                       mat[:, IDENT])
                        last.then_inc(t_done, 1)

                    def column_modes(i, s):
                        pe.wait_ge(t_copied, i * PAIRS + GPS * (s + 1))
                        for ki in range(KI):
                            for n in range(2 * WB):
                                k, ri = n // 2, n % 2
                                m = (ki * 2 + ri) * KB
                                last = nc.tensor.matmul(
                                    m_ps[s][:, ki * 2 * M2:(ki + 1) * 2 * M2],
                                    zt[:, s, k, m:m + KB, :], basis_w[:, k, ri],
                                    start=(n == 0), stop=(n == 2 * WB - 1))
                        last.then_inc(m_done, 1)

                    with pe.Fori(0, B // 2) as i:
                        for u in range(PAIRS):
                            row_modes(i, u)
                            if u:
                                transpose(i, u - 1)
                            if u == GPS + 1:
                                column_modes(i, 0)
                        transpose(i, PAIRS - 1)
                        column_modes(i, 1)

                @block.scalar
                def _(act):
                    def copy_z(i, u):
                        act.wait_ge(z_done, i * PAIRS + u + 1)
                        nc.scalar.copy(z[:, u % 2], z_ps[u % 2][:]).then_inc(z_copied, 1)

                    def copy_t(i, u):
                        act.wait_ge(t_done, i * PAIRS + u + 1)
                        g = u % GPS
                        nc.scalar.copy(
                            zt[:, u // GPS, :, :, 2 * g:2 * g + 2].rearrange("p k m c -> p (k m) c"),
                            t_ps[u % 2][:].rearrange("p k (c m) -> p k m c", c=2)).then_inc(t_copied, 1)

                    def copy_m(i, s):
                        act.wait_ge(m_done, i * 2 + s + 1)
                        nc.scalar.copy(modes_x[:, i * 2 + s], m_ps[s][:])

                    with act.Fori(0, B // 2) as i:
                        for u in range(PAIRS):
                            copy_z(i, u)
                            if u:
                                copy_t(i, u - 1)
                            if u == GPS + 2:
                                copy_m(i, 0)
                        copy_t(i, PAIRS - 1)
                        copy_m(i, 1)

                @block.vector
                def _(dve):
                    def aggregate(i, u):
                        dve.wait_ge(bn_done, i * PAIRS + u + 1)
                        dve.sem_inc(agg_begun, 1)
                        for ch in range(2):
                            last = nc.vector.bn_aggr(two_stats[:, u // GPS, 2 * (u % GPS) + ch],
                                                     bn[:, u % 2, ch].rearrange("p j k -> p (j k)"))
                        last.then_inc(bn_agg, 1)

                    with dve.Fori(0, B // 2) as i:
                        for u in range(PAIRS):
                            dve.wait_ge(x_in[u % LOADS], i * (16 * PAIRS // LOADS) + 16 * (u // LOADS + 1))
                            if u >= 2:
                                dve.wait_ge(bn_agg, i * PAIRS + u - 1)
                            for ch in range(2):
                                for j in range(HB):
                                    last = nc.vector.bn_stats(bn[:, u % 2, ch, j],
                                                              x_pair[:, u % LOADS, ch, j * W:(j + 1) * W])
                            last.then_inc(bn_done, 1)
                            if u:
                                aggregate(i, u - 1)
                        aggregate(i, PAIRS - 1)
                        dve.wait_ge(bn_agg, i * PAIRS + PAIRS)
                        nc.vector.tensor_copy(chan_stats[:, ds(i * 2, 2)], two_stats[:]).then_inc(stats_kept, 1)
                        dve.wait_ge(stats_kept, i + 1)

        pm = ExitStack()
        with pm:
            def sb(name, shape, dt=F32):
                return pm.enter_context(nc.sbuf_tensor(name, shape, dt))

            HALF = M2 // 2
            signed = sb("signed", [P, KI, M2, 3, B])
            coeff = sb("coeff", [C, 2, 2, M2, KB * C])
            mixer = sb("mixer", [P, 2, HALF, 2, P])
            proj_in = sb("proj_in", [C, C])
            proj_t = sb("proj_t", [C, C])
            weights_m = sb("weights_m", [P, 2, MODES])
            means = sb("means", [P, B * C])
            gmean = sb("gmean", [P, B, GPS])
            dev = sb("dev", [P, 3, B, C])
            dev4 = sb("dev4", [P, 3, B, KB, C])
            col = sb("col", [P, 3, B])
            vec = sb("vec", [P, 16, B])
            prod = signed[:].rearrange("p k j s b -> p (k j s b)")[:, 0:B * MODES].rearrange(
                "p (b m) -> p b m", b=B)
            w_in = sb("w_in", [P, C, TAPS * TAPS])
            w_scaled = sb("w_scaled", [P, TAPS * TAPS, C])
            w_t = sb("w_t", [P, TAPS * TAPS, C])
            w_part = sb("w_part", [P, 2, TAPS * TAPS, C], F16)
            w_max = sb("w_max", [P, 4])
            cols_basis = sb("cols_basis", [P, W])
            stat_ps = pm.enter_context(nc.psum_tensor("stat_ps", [P, 512], F32))
            w_ps = [pm.enter_context(nc.psum_tensor(f"w_ps{i}", [P, 2, HALF * C], F32)) for i in range(2)]
            y_ps = [pm.enter_context(nc.psum_tensor(f"y_ps{i}", [P, M2, 2, B], F32)) for i in range(2)]

            small_in, mode_w_in, conv_in = sem("small_in"), sem("mode_w_in"), sem("conv_in")
            coeff_in = [sem(f"coeff_in{i}") for i in range(2)]
            step = sem("step")
            to_pe = sem("to_pe")
            from_pe = sem("from_pe")
            to_act, from_act = sem("to_act"), sem("from_act")
            proj_ready, signed_ready, zeroed = sem("proj_ready"), sem("signed_ready"), sem("zeroed")
            w_done, mix_done = sem("w_done"), sem("mix_done")
            act_placed, dve_placed, y_copied = sem("act_placed"), sem("dve_placed"), sem("y_copied")

            co = [a.rearrange("r (m k) j c -> k m r j c", m=KB) for a in (coeff_re, coeff_im)]
            NSTEP = 4
            (FIRST_MEAN, COLS, VAR0, DC, VAR1, BOUND) = range(1, 7)

            with nc.Block() as block:
                @block.sync
                def _(sp):
                    sp.dma_start(proj_in[:], proj).then_inc(small_in, 16)
                    for k in range(KB):
                        sp.dma_start(w_in[k * C:(k + 1) * C], weight.rearrange("o c s t -> o c (s t)")
                                     ).then_inc(conv_in, 16)
                    def load_coeff(ki, r):
                        for part in range(2):
                            for m in range(KB):
                                sp.dma_start(coeff[:, r, part, :, m * C:(m + 1) * C], co[part][ki, m]
                                             ).then_inc(coeff_in[r], 16)

                    load_coeff(0, 0)
                    load_coeff(1, 1)
                    sp.dma_start(weights_m[:], mode_weights).then_inc(mode_w_in, 16)
                    sp.dma_start(cols_basis[:], idft_w).then_inc(mode_w_in, 16)
                    sp.dma_start(rows_basis[:], idft_h).then_inc(mode_w_in, 16)
                    with sp.Fori(0, KI // 2 - 1) as i:
                        for r in range(2):
                            sp.wait_ge(w_done, i * NSTEP + 2 * r + 2)
                            load_coeff(i * 2 + r + 2, r)

                @block.gpsimd
                def _(pool):
                    for n, t in enumerate((mixer[:, 0], mixer[:, 1], taps[:], cols_lo[:])):
                        if n:
                            pool.wait_ge(zeroed, n)
                        nc.gpsimd.memset(t, 0.0).then_inc(zeroed, 1)

                @block.tensor
                def _(pe):
                    def small(n, cols, lhs, rhs, start=True, stop=True):
                        return nc.tensor.matmul(stat_ps[:, cols:cols + n], lhs, rhs, start=start, stop=stop)

                    small(B * C, 0, mat[:, MEAN], chan_stats[:, :, :, 0].rearrange("p b c -> p (b c)")
                          ).then_inc(from_pe, 1)
                    pe.wait_ge(to_pe, 1)
                    for k in range(3):
                        for b in range(B):
                            last = small(1, 256 + k * B + b, dev4[:, k, b].rearrange("p m c -> p (m c)"),
                                         mat[:, MEAN, 0:1])
                    last.then_inc(from_pe, 1)
                    pe.wait_ge(to_pe, 2)
                    small(B, 320, mat[:, PAIR], col[:, 1]).then_inc(from_pe, 1)

                    def project(i, n):
                        r = n // 2
                        if n % 2 == 0:
                            pe.wait_ge(coeff_in[r], i * (32 * KB) + 32 * KB)
                        if n >= 2:
                            pe.wait_ge(act_placed, i * NSTEP + n - 1)
                            pe.wait_ge(dve_placed, i * NSTEP + n - 1)
                        for k in range(HALF):
                            k2 = (n % 2) * HALF + k
                            for part in range(2):
                                at = (k * 2 + part) * C
                                last = nc.tensor.matmul(
                                    w_ps[n % 2][:, at // (HALF * C), at % (HALF * C):at % (HALF * C) + C],
                                    coeff[:, r, part, k2], proj_t[:],
                                    start=True, stop=True)
                        last.then_inc(w_done, 1)

                    def mix(i, n):
                        pe.wait_ge(act_placed, i * NSTEP + n + 1)
                        pe.wait_ge(dve_placed, i * NSTEP + n + 1)
                        for k in range(HALF):
                            k2 = (n % 2) * HALF + k
                            for part in range(2):
                                last = nc.tensor.matmul(
                                    y_ps[n // 2][:, k2].rearrange("p r b -> p (r b)"),
                                    mixer[:, n % 2, k, part],
                                    signed[:, i * 2 + n // 2, k2, 1 - part:3 - part, :],
                                    start=(part == 0), stop=(part == 1))
                        last.then_inc(mix_done, 1)

                    pe.wait_ge(proj_ready, 1)
                    pe.wait_ge(signed_ready, 1)
                    with pe.Fori(0, KI // 2) as i:
                        project(i, 0)
                        for n in range(1, NSTEP):
                            project(i, n)
                            mix(i, n - 1)
                        mix(i, NSTEP - 1)
                        pe.wait_ge(y_copied, i * 2 + 2)

                    pe.wait_ge(to_pe, 3)
                    small(B, 0, mat[:, DC_DEV], vec[:, 6])
                    small(B, 16, mat[:, DC_PAIR], vec[:, 6]).then_inc(from_pe, 1)
                    pe.wait_ge(to_pe, 4)
                    small(B, 32, mat[:, PAIR_ALL], vec[:, 9], stop=False)
                    small(B, 32, mat[:, PAIR], vec[:, 8], start=False, stop=False)
                    small(B, 32, mat[:, PAIR], col[:, 1], start=False).then_inc(from_pe, 1)
                    pe.wait_ge(to_pe, 5)
                    small(B, 64, mat[:, CHAN], vec[:, 12]).then_inc(from_pe, 1)

                @block.scalar
                def _(act):
                    act.wait_ge(to_act, 1)
                    nc.scalar.activation(vec[:, 1], vec[:, 0], ACT.Sqrt).then_inc(from_act, 1)
                    act.wait_ge(zeroed, 2)

                    with act.Fori(0, KI // 2) as i:
                        def place(n):
                            act.wait_ge(w_done, i * NSTEP + n + 1)
                            for m in range(KB):
                                last = nc.scalar.copy(
                                    mixer[m * C:(m + 1) * C, n % 2, 0:HALF // 2, :, m * C:(m + 1) * C],
                                    w_ps[n % 2][m * C:(m + 1) * C, 0])
                            last.then_inc(act_placed, 1)

                        def copy_y(r):
                            act.wait_ge(mix_done, i * NSTEP + 2 * r + 2)
                            at = i * 2 + r
                            nc.scalar.copy(
                                modes_y[:, :, ds(at * 2 * M2, 2 * M2)].rearrange("p b (r j) -> p j r b", r=2),
                                y_ps[r][:]).then_inc(y_copied, 1)

                        place(0)
                        place(1)
                        act.wait_ge(mix_done, i * NSTEP + 1)
                        place(2)
                        act.wait_ge(mix_done, i * NSTEP + 2)
                        copy_y(0)
                        place(3)
                        copy_y(1)

                    for n in range(2):
                        act.wait_ge(to_act, 2 + n)
                        nc.scalar.activation(vec[:, 1], vec[:, 0], ACT.Sqrt).then_inc(from_act, 1)

                @block.vector
                def _(dve):
                    count = [0, 0, 0]

                    def done(ins):
                        count[0] += 1
                        ins.then_inc(step, 1)
                        dve.wait_ge(step, count[0])

                    def tt(o, a, b, op):
                        done(nc.vector.tensor_tensor(o, a, b, op))

                    def ts(o, a, s1, s2, op0, op1=None):
                        if op1 is None:
                            done(nc.vector.tensor_scalar(o, a, s1, None, op0))
                        else:
                            done(nc.vector.tensor_scalar(o, a, s1, s2, op0, op1))

                    def give_pe():
                        count[1] += 1
                        nc.vector.tensor_copy(vec[:, 15, 0:1], vec[:, 15, 1:2]).then_inc(to_pe, 1)

                    def root(v, k):
                        done(nc.vector.tensor_copy(vec[:, 0], v))
                        nc.vector.tensor_copy(vec[:, 15, 0:1], vec[:, 15, 1:2]).then_inc(to_act, 1)
                        dve.wait_ge(from_act, k)
                        done(nc.vector.reciprocal(vec[:, 2], vec[:, 1]))
                        tt(vec[:, 2], vec[:, 2], vec[:, 0], ALU.mult)
                        tt(vec[:, 2], vec[:, 2], vec[:, 1], ALU.add)
                        ts(vec[:, 2], vec[:, 2], 0.5, None, ALU.mult)

                    done(nc.vector.memset(vec[:], 0.0))
                    dve.wait_ge(small_in, 16)
                    nc.vector.transpose(proj_t[:], proj_in[:]).then_inc(proj_ready, 1)

                    dve.wait_ge(from_pe, FIRST_MEAN)
                    done(nc.vector.tensor_copy(means[:], stat_ps[:, 0:B * C]))
                    mv = means[:].rearrange("p (b g i) -> p b g i", b=B, i=2)
                    tt(gmean[:], mv[:, :, :, 0], mv[:, :, :, 1], ALU.add)
                    ts(gmean[:], gmean[:], 0.5, None, ALU.mult)
                    gb = gmean[:].rearrange("p b g -> p (b g)").unsqueeze(2).broadcast_to([P, B * GPS, 2])
                    fl = lambda k: dev[:, k].rearrange("p b (g i) -> p (b g) i", i=2)
                    cs = lambda k: chan_stats[:, :, :, k].rearrange("p b (g i) -> p (b g) i", i=2)
                    tt(fl(0), cs(0), gb, ALU.subtract)
                    tt(fl(1), fl(0), fl(0), ALU.mult)
                    tt(fl(1), fl(1), cs(1), ALU.add)
                    done(nc.vector.tensor_copy(fl(2), gb))
                    for m in range(KB):
                        done(nc.vector.tensor_copy(dev4[:, :, :, m].rearrange("p k b c -> p (k b) c"),
                                                   dev[:].rearrange("p k b c -> p (k b) c")))
                    give_pe()
                    dve.wait_ge(from_pe, COLS)
                    done(nc.vector.tensor_copy(col[:].rearrange("p k b -> p (k b)"),
                                               stat_ps[:, 256:256 + 3 * B]))
                    give_pe()
                    dve.wait_ge(from_pe, VAR0)
                    ts(vec[:, 3], stat_ps[:, 320:320 + B], GN_EPS, None, ALU.add)
                    root(vec[:, 3], 1)
                    done(nc.vector.reciprocal(vec[:, 4], vec[:, 2]))
                    ts(vec[:, 5], vec[:, 4], -1.0, None, ALU.mult)
                    ts(modes_x[0:C, :, 0], col[0:C, 0], float(HW), None, ALU.mult)

                    for b in range(B):
                        mx = modes_x[:, b].rearrange("p (k r j) -> p k r j", k=KI, r=2)
                        for s, (ri, v) in enumerate(((1, 5), (0, 4), (1, 4))):
                            done(nc.vector.tensor_scalar(signed[:, :, :, s, b], mx[:, :, ri],
                                                         vec[:, v, b:b + 1], None, ALU.mult))
                    nc.vector.tensor_copy(vec[:, 15, 0:1], vec[:, 15, 1:2]).then_inc(signed_ready, 1)
                    dve.wait_ge(zeroed, 4)

                    with dve.Fori(0, KI // 2) as i:
                        def place(n):
                            dve.wait_ge(w_done, i * NSTEP + n + 1)
                            for m in range(KB):
                                last = nc.vector.tensor_copy(
                                    mixer[m * C:(m + 1) * C, n % 2, HALF // 2:HALF, :, m * C:(m + 1) * C],
                                    w_ps[n % 2][m * C:(m + 1) * C, 1].rearrange("p (k r c) -> p k r c", r=2, c=C))
                            last.then_inc(dve_placed, 1)

                        place(0)
                        place(1)
                        dve.wait_ge(mix_done, i * NSTEP + 1)
                        place(2)
                        dve.wait_ge(mix_done, i * NSTEP + 2)
                        place(3)
                        dve.wait_ge(mix_done, i * NSTEP + 4)

                    dve.wait_ge(y_copied, KI)
                    dve.wait_ge(mode_w_in, 48)
                    done(nc.vector.tensor_copy(vec[:, 6], modes_y[:, :, 0]))
                    give_pe()
                    for k, other in ((0, modes_x), (1, modes_y)):
                        tt(prod, modes_y[:], other[:], ALU.mult)
                        tt(prod, prod, weights_m[:, k:k + 1].broadcast_to([P, B, MODES]), ALU.mult)
                        done(nc.vector.tensor_reduce(vec[:, 9 + k], prod, AX.X, ALU.add))
                    done(nc.vector.scalar_tensor_tensor(vec[:, 9], vec[:, 9], 2.0, vec[:, 10], ALU.mult, ALU.add))
                    dve.wait_ge(from_pe, DC)
                    done(nc.vector.tensor_copy(vec[:, 7], stat_ps[:, 0:B]))
                    tt(vec[:, 11], stat_ps[:, 16:16 + B], col[:, 2], ALU.add)
                    done(nc.vector.scalar_tensor_tensor(vec[:, 8], col[:, 0], 2.0, vec[:, 7], ALU.mult, ALU.add))
                    tt(vec[:, 8], vec[:, 8], vec[:, 7], ALU.mult)
                    give_pe()
                    dve.wait_ge(from_pe, VAR1)
                    ts(vec[:, 3], stat_ps[:, 32:32 + B], 0.0, GN_EPS, ALU.max, ALU.add)
                    root(vec[:, 3], 2)
                    done(nc.vector.reciprocal(vec[:, 4], vec[:, 2]))
                    ts(scalars[:, :, GAIN], vec[:, 4], G_SCALE, None, ALU.mult)
                    done(nc.vector.tensor_copy(scalars[:, :, SHIFT], vec[:, 11]))
                    done(nc.vector.scalar_tensor_tensor(modes_y[0:C, :, 0], vec[0:C, 11], -float(HW),
                                                        modes_y[0:C, :, 0], ALU.mult, ALU.add))
                    tt(prod, modes_y[:], modes_y[:], ALU.mult)
                    done(nc.vector.tensor_reduce(vec[:, 12], prod, AX.X, ALU.add))
                    give_pe()
                    dve.wait_ge(from_pe, BOUND)
                    ts(vec[:, 3], stat_ps[:, 64:64 + B], float(M1), TINY, ALU.mult, ALU.max)
                    root(vec[:, 3], 3)
                    ts(scalars[:, :, ALPHA], vec[:, 2], 1.0 / (Y_SCALE * HW), None, ALU.mult)
                    done(nc.vector.reciprocal(vec[:, 4], vec[:, 2]))
                    ts(scalars[:, :, 3], vec[:, 4], Y_SCALE, None, ALU.mult)
                    for b in range(B):
                        done(nc.vector.tensor_scalar(modes_y[:, b], modes_y[:, b], scalars[:, b, 3:4], None,
                                                     ALU.mult))

                    done(nc.vector.tensor_copy(cols_hi[:], cols_basis[:]))
                    tt(cols_lo[0:64], cols_basis[0:64], cols_hi[0:64], ALU.subtract)

                    dve.wait_ge(conv_in, 16 * KB)
                    flat = w_in[:].rearrange("p c t -> p (c t)")
                    done(nc.vector.tensor_reduce(w_max[:, 0:1], flat, AX.X, ALU.max))
                    done(nc.vector.tensor_reduce(w_max[:, 1:2], flat, AX.X, ALU.min))
                    ts(w_max[:, 1:2], w_max[:, 1:2], -1.0, TINY, ALU.mult, ALU.max)
                    tt(w_max[:, 0:1], w_max[:, 0:1], w_max[:, 1:2], ALU.max)
                    ts(unscale[:], w_max[:, 0:1], 1.0 / (W_SCALE * G_SCALE), None, ALU.mult)
                    done(nc.vector.reciprocal(w_max[:, 2:3], w_max[:, 0:1]))
                    ts(w_scaled[:], w_in[:].rearrange("p c t -> p t c"), w_max[:, 2:3], W_SCALE, ALU.mult, ALU.mult)
                    done(nc.vector.transpose(w_t[:].rearrange("p t c -> p (t c)"),
                                             w_scaled[:].rearrange("p t c -> p (t c)")))
                    done(nc.vector.tensor_copy(w_part[:, 0], w_t[:]))
                    tt(w_part[:, 1], w_t[:], w_part[:, 0], ALU.subtract)
                    for first, kb, mb, s in tap_blocks():
                        for part in range(2):
                            nc.vector.tensor_copy(
                                taps[kb * C:(kb + 1) * C, part, first, :, mb * C:(mb + 1) * C],
                                w_part[kb * C:(kb + 1) * C, part, s * TAPS:(s + 1) * TAPS])

        before_c.close()
        pc = ExitStack()
        with pc:
            def sb(name, shape, dt=F32):
                return pc.enter_context(nc.sbuf_tensor(name, shape, dt))

            GW = W + TAPS - 1
            x_ring = sb("x_ring", [P, RING, SLOTS, W])
            x_edge = sb("x_edge", [P, W])
            g_ring = sb("g_ring", [P, RING, SLOTS, 2, GW], F16)
            g_edge = sb("g_edge", [P, 2, GW], F16)
            o_ring = sb("o_ring", [P, 2, SLOTS, W])
            row_modes = sb("row_modes", [P, 2, (Q + 1) * KB, C], F16)
            y_src = sb("y_src", [P, M2, 2, KI, 4])
            y_t = sb("y_t", [P, 2 * M2, C])
            y_one = sb("y_one", [P, 2, 2 * M2])
            cur = sb("cur", [P, 2, 4])
            conv_ps = [pc.enter_context(nc.psum_tensor(f"conv_ps{i}", [P, W], F32)) for i in range(2)]
            add_ps = [pc.enter_context(nc.psum_tensor(f"add_ps{i}", [P, 2, W], F32)) for i in range(2)]
            row_ps = pc.enter_context(nc.psum_tensor("row_ps", [P, W], F32))
            tail_ps = pc.enter_context(nc.psum_tensor("tail_ps", [P, KB], F32))

            xl = [sem(f"xl{i}") for i in range(RING)]
            xl_edge = sem("xl_edge")
            add_done = sem("add_done")
            x1_ready = sem("x1_ready")
            hi_ready, lo_ready = sem("hi_ready"), sem("lo_ready")
            g_ready = sem("g_ready")
            conv_done, evac_done = sem("conv_done"), sem("evac_done")
            res_done = sem("res_done")
            stored = [sem(f"stored{i}") for i in range(2)]
            src_ready, one_ready = sem("src_ready"), sem("one_ready")
            rows_done, rows_hi, rows_lo = sem("rows_done"), sem("rows_hi"), sem("rows_lo")
            cstep = sem("cstep")
            borders_begun = sem("borders_begun")

            HALVES = 2 * NCH + 1
            CHUNKS = NCH + 1
            XB = 64
            xv = x.rearrange("b c (q m) w -> b m c q w", m=KB)
            ov = out.rearrange("b c (q m) w -> b m c q w", m=KB)
            TURNS = NCH // RING

            def blk(m):
                return slice(m * C, (m + 1) * C)

            def channels_at(n):
                extra = {NCH - 4: (NCH - 4, NCH - 3), NCH - 3: (NCH - 2, NCH - 1)}
                return extra.get(n, ())

            def samples(eng, body):
                if B > 2:
                    with eng.Fori(0, B // 2 - 1) as i:
                        body(i * 2, 0, True)
                        body(i * 2 + 1, 1, True)
                body(B - 2, 0, True)
                body(B - 1, 1, False)

            def steps(eng, one):
                with eng.Fori(0, TURNS - 1) as i:
                    for k in range(RING):
                        one(i * RING + k, i, k, False)
                for k in range(RING):
                    one(NCH - RING + k, TURNS - 1, k, True)

            def half_bank(par, h):
                return (par * HALVES + h) % 2

            with nc.Block() as block:
                @block.sync
                def _(sp):
                    def load(b, n, k):
                        for m in range(KB - 1):
                            sp.dma_start(x_ring[blk(m), k], xv[b, m, :, ds(n * SLOTS, SLOTS)]).then_inc(xl[k], 16)
                        sp.dma_start(x_ring[blk(3), k], xv[b, 3, :, ds(n * SLOTS - 1, SLOTS)]).then_inc(xl[k], 16)

                    def load_first(b):
                        for m in range(KB - 1):
                            sp.dma_start(x_ring[blk(m), 0], xv[b, m, :, 0:SLOTS]).then_inc(xl[0], 16)
                        sp.dma_start(x_ring[blk(3), 0, 0], xv[b, 1, :, 0]).then_inc(xl[0], 16)
                        sp.dma_start(x_ring[blk(3), 0, 1:SLOTS], xv[b, 3, :, 0:SLOTS - 1]).then_inc(xl[0], 16)

                    def load_edge(b):
                        for m, (q, r) in enumerate(((Q - 1, 2), (Q - 1, 1), (0, 2), (Q - 1, 3))):
                            sp.dma_start(x_edge[blk(m)], xv[b, r, :, q]).then_inc(xl_edge, 16)

                    def sample(b, par, has_next):
                        load_edge(b)

                        def one(n, i, k, last):
                            if not last or k == 0:
                                load(b, n + 3, (k + 3) % RING)
                            elif has_next:
                                if k == 1:
                                    load_first(b + 1)
                                else:
                                    load(b + 1, k - 1, k - 1)
                            sp.wait_ge(res_done, b * NCH + n + 1)
                            for m in range(KB):
                                sp.dma_start(ov[b, m, :, ds(n * SLOTS, SLOTS)], o_ring[blk(m), k % 2]
                                             ).then_inc(stored[k % 2], 16)
                        steps(sp, one)

                    load_first(0)
                    load(0, 1, 1)
                    load(0, 2, 2)
                    samples(sp, sample)
                    for r in range(2):
                        sp.wait_ge(stored[r], XB + XB * B * NCH // 2)

                @block.gpsimd
                def _(pool):
                    def borders(g):
                        pool.sem_inc(borders_begun, 1)
                        nc.gpsimd.tensor_copy(g[:, :, 0:GW:GW - 1], g[:, :, 2:4]).then_inc(g_ready, 1)
                        nc.gpsimd.tensor_copy(g[:, :, W + 1:W + 2], g[:, :, W - 1:W]).then_inc(g_ready, 1)
                        nc.gpsimd.tensor_copy(g[:, :, W + 2:W + 3], g[:, :, W - 2:W - 1]).then_inc(g_ready, 1)

                    def chunk(b, n, k):
                        pool.wait_ge(hi_ready, b * HALVES + n * 2 + 2)
                        pool.wait_ge(lo_ready, b * HALVES + n * 2 + 2)
                        borders(g_ring[:, k].rearrange("p s h w -> p (s h) w"))

                    def sample(b, par, has_next):
                        def one(n, i, k, last):
                            if last and k == RING - 1:
                                pool.wait_ge(hi_ready, b * HALVES + HALVES)
                                pool.wait_ge(lo_ready, b * HALVES + HALVES)
                                borders(g_edge[:])
                                if has_next:
                                    chunk(b + 1, 0, 0)
                            else:
                                chunk(b, n + 1, (k + 1) % RING)
                        steps(pool, one)

                    chunk(0, 0, 0)
                    samples(pool, sample)

                @block.tensor
                def _(pe):
                    def add_half(b, par, n, k, h):
                        bank = half_bank(par, 2 * k + h)
                        if not (isinstance(b, int) and b == 0 and isinstance(n, int) and n == 0):
                            pe.wait_ge(x1_ready, b * HALVES + n * 2 + h - 1)
                        for j in range(2):
                            at = n * (SLOTS * P) + (2 * h + j) * P
                            for basis, first in ((cols_hi, True), (cols_lo, False)):
                                last = nc.tensor.matmul(
                                    add_ps[bank][:, j],
                                    row_modes[:, par].rearrange("p r c -> p (r c)")[:, ds(at, P)],
                                    basis[:], start=first, stop=not first)
                        last.then_inc(add_done, 1)

                    def add_edge(b, par):
                        bank = half_bank(par, 2 * NCH)
                        pe.wait_ge(x1_ready, b * HALVES + HALVES - 2)
                        for basis, first in ((cols_hi, True), (cols_lo, False)):
                            last = nc.tensor.matmul(add_ps[bank][:, 0], row_modes[:, par, Q * KB:(Q + 1) * KB],
                                                    basis[:], start=first, stop=not first)
                        last.then_inc(add_done, 1)

                    def rows(b, o):
                        pe.wait_ge(one_ready, b * C + o + 1)
                        pe.wait_ge(rows_lo, b * C + o + 1)
                        lhs = y_one[:].rearrange("p d m -> p (d m)")
                        nc.tensor.matmul(row_ps[:], lhs, rows_basis[:, 0:Q * KB], start=True, stop=True)
                        nc.tensor.matmul(tail_ps[:], lhs, rows_basis[:, Q * KB:(Q + 1) * KB],
                                         start=True, stop=True).then_inc(rows_done, 1)

                    def conv(b, n, k, j, upper, lower):
                        pe.wait_ge(evac_done, b * Q + n * SLOTS + j + 1)
                        todo = []
                        for first, g in ((0, upper), (1, lower)):
                            for t in range(TAPS):
                                w = slice(TAPS - 1 - t, TAPS - 1 - t + W)
                                todo += [(taps[:, 0, first, t], g[:, 0, w]), (taps[:, 0, first, t], g[:, 1, w]),
                                         (taps[:, 1, first, t], g[:, 0, w])]
                        for e, (lhs, rhs) in enumerate(todo):
                            last = nc.tensor.matmul(conv_ps[j % 2][:], lhs, rhs, start=(e == 0),
                                                    stop=(e == len(todo) - 1))
                        last.then_inc(conv_done, 1)

                    def sample(b, par, has_next):
                        def one(n, i, k, last):
                            final = last and k == RING - 1
                            if final:
                                add_edge(b, par)
                                if has_next:
                                    for h in range(2):
                                        add_half(b + 1, 1 - par, 0, 0, h)
                            else:
                                for h in range(2):
                                    add_half(b, par, n + 1, (k + 1) % RING, h)
                            for j in range(SLOTS):
                                if j == 0:
                                    pe.wait_ge(g_ready, b * (3 * CHUNKS) + n * 3 + 3)
                                if j == SLOTS - 1:
                                    pe.wait_ge(g_ready, b * (3 * CHUNKS) + n * 3 + 6)
                                upper = g_ring[:, k, j]
                                lower = (g_ring[:, k, j + 1] if j < SLOTS - 1 else
                                         g_edge[:] if final else g_ring[:, (k + 1) % RING, 0])
                                conv(b, n, k, j, upper, lower)
                                if has_next:
                                    if not last and j == 1:
                                        rows(b + 1, n)
                                    if last and j in (1, 2) and channels_at(n):
                                        rows(b + 1, channels_at(n)[j - 1])
                        steps(pe, one)

                    with pe.Fori(0, C) as o:
                        rows(0, o)
                    pe.wait_ge(rows_lo, C + 1)
                    for h in range(2):
                        add_half(0, 0, 0, 0, h)
                    samples(pe, sample)

                @block.scalar
                def _(act):
                    def rows(b, par, o):
                        act.wait_ge(rows_done, b * C + o + 1)
                        nc.scalar.copy(row_modes[:, par, 0:Q * KB, ds(o, 1)].rearrange("p r c -> p (r c)"),
                                       row_ps[:])
                        nc.scalar.copy(row_modes[:, par, Q * KB:(Q + 1) * KB, ds(o, 1)].rearrange("p r c -> p (r c)"),
                                       tail_ps[:]).then_inc(rows_hi, 1)

                    def high(b, par, n, k, h):
                        act.wait_ge(x1_ready, b * HALVES + n * 2 + h + 1)
                        s = slice(2 * h, 2 * h + 2)
                        nc.scalar.activation(g_ring[:, k, s, 0, 1:W + 1], x_ring[:, k, s], ACT.Copy,
                                             scale=cur[:, par, GAIN:GAIN + 1]).then_inc(hi_ready, 1)

                    def high_edge(b, par):
                        act.wait_ge(x1_ready, b * HALVES + HALVES)
                        nc.scalar.activation(g_edge[:, 0, 1:W + 1], x_edge[:], ACT.Copy,
                                             scale=cur[:, par, GAIN:GAIN + 1]).then_inc(hi_ready, 1)

                    def sample(b, par, has_next):
                        def one(n, i, k, last):
                            if last and k == RING - 1:
                                high_edge(b, par)
                                if has_next:
                                    for h in range(2):
                                        high(b + 1, 1 - par, 0, 0, h)
                            else:
                                for h in range(2):
                                    high(b, par, n + 1, (k + 1) % RING, h)
                            act.wait_ge(stored[k % 2], b * (XB * NCH // 2) + i * (XB * RING // 2) + XB * (k // 2) + XB)
                            for j in range(SLOTS):
                                act.wait_ge(conv_done, b * Q + n * SLOTS + j + 1)
                                nc.scalar.activation(o_ring[:, k % 2, j], conv_ps[j % 2][:], ACT.Identity,
                                                     scale=unscale[:], bias=cur[:, par, SHIFT:SHIFT + 1]
                                                     ).then_inc(evac_done, 1)
                                if has_next:
                                    if not last and j == 1:
                                        rows(b + 1, 1 - par, n)
                                    if last and j in (1, 2) and channels_at(n):
                                        rows(b + 1, 1 - par, channels_at(n)[j - 1])
                        steps(act, one)

                    act.sem_inc(evac_done, 2)
                    for r in range(2):
                        act.sem_inc(stored[r], XB)
                    with act.Fori(0, C) as o:
                        rows(0, 0, o)
                    for h in range(2):
                        high(0, 0, 0, 0, h)
                    samples(act, sample)

                @block.vector
                def _(dve):
                    def source(b, par):
                        nc.vector.tensor_copy(cur[:, par], scalars[:, b])
                        my = modes_y[:, b].rearrange("p (k r j) -> p j k r", k=KI, r=2)
                        for t, s, r, sign in ((0, 0, 0, 1.0), (0, 1, 1, -1.0), (1, 0, 1, 1.0), (1, 1, 0, 1.0)):
                            last = nc.vector.tensor_scalar(y_src[:, :, t, :, s], my[:, :, :, r], sign, None, ALU.mult)
                        last.then_inc(cstep, 1)
                        dve.wait_ge(cstep, b * 2 + 2)
                        nc.vector.transpose(y_t[:].rearrange("p m c -> p (m c)"),
                                            y_src[:].rearrange("p j t k s -> p (j t k s)")).then_inc(cstep, 1)

                    def one_channel(b, o):
                        dve.wait_ge(cstep, b * 2 + 3)
                        nc.vector.tensor_copy(
                            y_one[:], y_t[:, :, ds(o, 1)].rearrange("p m c -> p c m").broadcast_to([P, 2, 2 * M2])
                        ).then_inc(one_ready, 1)

                    def low_rows(b, par, o):
                        dve.wait_ge(rows_hi, b * C + o + 1)
                        lo = slice(64, P)
                        for r, ps in ((slice(0, Q * KB), row_ps), (slice(Q * KB, (Q + 1) * KB), tail_ps)):
                            ap = row_modes[lo, par, r, ds(o, 1)].rearrange("p r c -> p (r c)")
                            last = nc.vector.tensor_tensor(ap, ps[lo], ap, ALU.subtract)
                        last.then_inc(rows_lo, 1)

                    def add(b, par, n, i, k, h):
                        dve.wait_ge(add_done, b * HALVES + n * 2 + h + 1)
                        s = slice(2 * h, 2 * h + 2)
                        nc.vector.scalar_tensor_tensor(
                            x_ring[:, k, s].rearrange("p s w -> p (s w)"),
                            add_ps[half_bank(par, 2 * k + h)][:].rearrange("p s w -> p (s w)"),
                            cur[:, par, ALPHA:ALPHA + 1],
                            x_ring[:, k, s].rearrange("p s w -> p (s w)"), ALU.mult, ALU.add).then_inc(x1_ready, 1)

                    def low(b, par, n, k, h):
                        dve.wait_ge(hi_ready, b * HALVES + n * 2 + h + 1)
                        s = slice(2 * h, 2 * h + 2)
                        nc.vector.scalar_tensor_tensor(
                            g_ring[:, k, s, 1, 1:W + 1], x_ring[:, k, s], cur[:, par, GAIN:GAIN + 1],
                            g_ring[:, k, s, 0, 1:W + 1], ALU.mult, ALU.subtract).then_inc(lo_ready, 1)

                    def edge(b, par):
                        dve.wait_ge(xl_edge, b * 64 + 64)
                        dve.wait_ge(add_done, b * HALVES + HALVES)
                        nc.vector.scalar_tensor_tensor(
                            x_edge[:], add_ps[half_bank(par, 2 * NCH)][:, 0], cur[:, par, ALPHA:ALPHA + 1],
                            x_edge[:], ALU.mult, ALU.add).then_inc(x1_ready, 1)

                    def edge_low(b, par):
                        dve.wait_ge(hi_ready, b * HALVES + HALVES)
                        nc.vector.scalar_tensor_tensor(
                            g_edge[:, 1, 1:W + 1], x_edge[:], cur[:, par, GAIN:GAIN + 1],
                            g_edge[:, 0, 1:W + 1], ALU.mult, ALU.subtract).then_inc(lo_ready, 1)

                    def loaded(b, n, i, k):
                        per = XB * TURNS
                        if k == 0:
                            dve.wait_ge(xl[0], b * (per + 16) + i * XB + XB + 16)
                        else:
                            dve.wait_ge(xl[k], b * per + i * XB + XB)

                    def residual(b, n, k, final):
                        dve.wait_ge(evac_done, b * Q + n * SLOTS + SLOTS + 2)
                        o = o_ring[:, k % 2]
                        top3 = slice(0, 3 * C)
                        nc.vector.tensor_tensor(o[top3], o[top3], x_ring[top3, k], ALU.add)
                        nc.vector.tensor_tensor(o[blk(3), 0:SLOTS - 1], o[blk(3), 0:SLOTS - 1],
                                                x_ring[blk(3), k, 1:SLOTS], ALU.add)
                        nxt = x_edge[blk(3)] if final else x_ring[blk(3), (k + 1) % RING, 0]
                        nc.vector.tensor_tensor(o[blk(3), SLOTS - 1], o[blk(3), SLOTS - 1], nxt,
                                                ALU.add).then_inc(res_done, 1)

                    def sample(b, par, has_next):
                        if has_next:
                            source(b + 1, 1 - par)

                        def one(n, i, k, last):
                            final = last and k == RING - 1
                            if has_next and not last:
                                one_channel(b + 1, n)
                            if final:
                                edge(b, par)
                                edge_low(b, par)
                                if has_next:
                                    loaded(b + 1, 0, 0, 0)
                                    for h in range(2):
                                        add(b + 1, 1 - par, 0, 0, 0, h)
                                    for h in range(2):
                                        low(b + 1, 1 - par, 0, 0, h)
                            else:
                                k1 = (k + 1) % RING
                                loaded(b, n + 1, i + (k + 1) // RING, k1)
                                for h in range(2):
                                    add(b, par, n + 1, i, k1, h)
                                for h in range(2):
                                    low(b, par, n + 1, k1, h)
                            if has_next and not last:
                                low_rows(b + 1, 1 - par, n)
                            if has_next and last:
                                for o in channels_at(n):
                                    one_channel(b + 1, o)
                                    low_rows(b + 1, 1 - par, o)
                            residual(b, n, k, final)
                        steps(dve, one)

                    dve.sem_inc(rows_lo, 1)
                    nc.vector.memset(y_src[:], 0.0).then_inc(cstep, 1)
                    dve.wait_ge(cstep, 1)
                    source(0, 0)
                    with dve.Fori(0, C) as o:
                        one_channel(0, o)
                        low_rows(0, 0, o)
                    loaded(0, 0, 0, 0)
                    for h in range(2):
                        add(0, 0, 0, 0, 0, h)
                    for h in range(2):
                        low(0, 0, 0, 0, h)
                    samples(dve, sample)


def tap_blocks():
    found = []
    for first in range(2):
        for kb in range(KB):
            row_in = KB * first + (kb if kb < 3 else -1)
            for mb in range(KB):
                s = mb + 3 - row_in
                if 0 <= s < TAPS:
                    found.append((first, kb, mb, s))
    assert len(found) == KB * TAPS
    return found


def kernel(x, L0_conv_coeff_real, L0_conv_coeff_imag, L0_conv_proj, L1_conv_weight):
    import concourse.bacc as bacc
    from concourse.bass_utils import run_bass_kernel_spmd

    nc = bacc.Bacc("TRN2", target_bir_lowering=False, num_devices=1)
    data = dict(x=x, coeff_re=L0_conv_coeff_real, coeff_im=L0_conv_coeff_imag, proj=L0_conv_proj,
                weight=L1_conv_weight)
    arrays = {n: np.ascontiguousarray(a) for n, a in data.items()}
    arrays.update(constant_tables(*arrays["x"].shape[2:]))
    args = [nc.dram_tensor(n, list(a.shape), F32, kind="ExternalInput").ap() for n, a in arrays.items()]
    args.append(nc.dram_tensor("result", list(arrays["x"].shape), F32, kind="ExternalOutput").ap())
    two_conv_layers(nc, *args)
    return run_bass_kernel_spmd(nc, [arrays], core_ids=[0]).results[0]["result"]
```

```python
from contextlib import ExitStack

import numpy as np
import concourse.bass as bass
from concourse import mybir

F32 = mybir.dt.float32
F16 = mybir.dt.float16
ALU = mybir.AluOpType
ACT = mybir.ActivationFunctionType
AX = mybir.AxisListType

P = 128
C = 32
M1 = 32
M2 = 32
KB = P // C
KI = M1 // KB
TAPS = 5
MID, EVEN, ODD = (0, 3), (3, 3), (6, 2)
FILTER = 8
SLOTS = 4
RING = 4
G_SCALE = 32.0
W_SCALE = 1024.0
Y_SCALE = 16384.0
GN_EPS = 1e-5
TINY = 1e-30

IDENT, MEAN, PAIR, PAIR_ALL, DC_DEV, DC_PAIR, CHAN, FIRST_TWO, NO_CONST = range(9)
MATS = 9
ALPHA, GAIN, SHIFT = range(3)


def constant_tables(H, W):
    f = np.float64
    k1 = np.arange(M1).reshape(KB, KI)
    h = np.arange(H).reshape(P, H // P)
    ang = 2 * np.pi * h[:, :, None, None] * k1.T[None, None] / H
    dft_h = np.stack([np.cos(ang), -np.sin(ang)], axis=3).reshape(P, H // P, 2 * M1)
    w = np.arange(W).reshape(W // P, P).T
    ang = 2 * np.pi * w[:, :, None] * np.arange(M2) / W
    c, s = np.cos(ang), np.sin(ang)
    dft_w = np.stack([np.concatenate([c, -s], -1), np.concatenate([s, c], -1)], axis=2)
    Q = H // KB
    rows = np.empty((Q, KB), int)
    rows[:, :3] = KB * np.arange(Q)[:, None] + np.arange(3)
    rows[:, 3] = (KB * np.arange(Q) - 1) % H
    ang = 2 * np.pi * k1.reshape(-1, 1) * rows.reshape(1, -1) / H
    idft_h = np.stack([np.cos(ang), np.sin(ang)] * 2, axis=1)
    ang = 2 * np.pi * np.arange(M2)[:, None] * np.arange(W)[None] / W
    fold = np.where(np.arange(M2) == 0, 1.0, 2.0)[:, None]
    half = np.stack([fold * np.cos(ang), -fold * np.sin(ang)], axis=1).reshape(2 * M2, W)
    idft_w = np.concatenate([half, half])
    k = np.arange(P)[:, None]
    m = np.arange(P)[None]
    same_pair = (k % C) // 2 == (m % C) // 2
    mats = np.zeros((MATS, P, P))
    mats[IDENT] = k == m
    mats[MEAN] = 1.0 / P
    mats[PAIR] = 0.5 * (k // 2 == m // 2)
    mats[PAIR_ALL] = same_pair / (2.0 * (H * W) ** 2)
    mats[DC_PAIR] = (k < C) * same_pair * 0.5 / (H * W)
    mats[DC_DEV] = (k < C) * (k == m % C) / (H * W) - mats[DC_PAIR]
    mats[CHAN] = k % C == m % C
    mats[FIRST_TWO] = k % 4 < 2
    mats[NO_CONST] = k >= C
    out = dict(dft_h=dft_h, dft_w=dft_w.reshape(P, W // P, 2, 2 * M2), idft_h=idft_h.reshape(P, -1),
               idft_w=idft_w, mats=mats.transpose(1, 0, 2))
    return {n: np.ascontiguousarray(a, dtype=np.float32) for n, a in out.items()}


def two_conv_layers(nc, x, coeff_re, coeff_im, proj, weight, dft_h, dft_w, idft_h, idft_w, mats,
                    out):
    B, _, H, W = x.shape
    HW = H * W
    HB, WB = H // P, W // P
    Q = H // KB
    NCH = Q // SLOTS
    GPS = C // 2
    MODES = KI * 2 * M2
    ds = bass.ds
    assert B % 2 == 0 and NCH % RING == 0 and NCH == C

    top = ExitStack()
    with top:
        def sem(name):
            return top.enter_context(nc.semaphore(name))

        def keep(name, shape, dt=F32):
            return top.enter_context(nc.sbuf_tensor(name, shape, dt))

        scalars = keep("scalars", [P, B, 4])
        unscale = keep("unscale", [P, 1])
        taps = keep("taps", [P, 2, 2, FILTER, P], F16)
        rows_hi = keep("rows_hi", [P, H], F16)
        rows_lo = keep("rows_lo", [P, H], F16)
        cols_hi = keep("cols_hi", [P, W], F16)
        cols_lo = keep("cols_lo", [P, W], F16)

        modes_store = nc.dram_tensor("modes_store", [P, B, MODES], F32).ap()

        before_c = top.enter_context(ExitStack())

        def until_c(name, shape, dt=F32):
            return before_c.enter_context(nc.sbuf_tensor(name, shape, dt))

        modes_x = until_c("modes_x", [P, B, MODES])
        modes_y = until_c("modes_y", [P, B, MODES])
        chan_stats = until_c("chan_stats", [P, B, C, 2])
        mat = until_c("mat", [P, MATS, P])

        pa = ExitStack()
        with pa:
            def sb(name, shape, dt=F32):
                return pa.enter_context(nc.sbuf_tensor(name, shape, dt))

            LOADS = 4
            PAIRS = 2 * GPS
            x_pair = sb("x_pair", [P, LOADS, 2, HB * W])
            basis_h = sb("basis_h", [P, HB, 2 * M1])
            basis_w = sb("basis_w", [P, WB, 2, 2 * M2])
            z = sb("z", [P, 2, W])
            zt = sb("zt", [P, 2, WB, 2 * M1, C])
            bn = sb("bn", [P, 2, 2, HB, 6])
            two_stats = sb("two_stats", [P, 2, C, 2])
            z_ps = [pa.enter_context(nc.psum_tensor(f"z_ps{i}", [P, W], F32)) for i in range(2)]
            t_ps = [pa.enter_context(nc.psum_tensor(f"t_ps{i}", [P, WB, P], F32)) for i in range(2)]
            m_ps = [pa.enter_context(nc.psum_tensor(f"m_ps{i}", [P, MODES], F32)) for i in range(2)]

            const_in = sem("const_in")
            x_in = [sem(f"x_in{i}") for i in range(LOADS)]
            z_done, z_copied = sem("z_done"), sem("z_copied")
            t_done, t_copied = sem("t_done"), sem("t_copied")
            m_done = sem("m_done")
            agg_begun = sem("agg_begun")
            bn_done, bn_agg, stats_kept = sem("bn_done"), sem("bn_agg"), sem("stats_kept")

            xa = x.rearrange("b (g i) (p j) w -> b g p i (j w)", i=2, j=HB)
            NCONST = 3 * 16

            with nc.Block() as block:
                @block.sync
                def _(sp):
                    sp.dma_start(basis_h[:], dft_h).then_inc(const_in, 16)
                    sp.dma_start(basis_w[:], dft_w).then_inc(const_in, 16)
                    sp.dma_start(mat[:], mats).then_inc(const_in, 16)
                    for n in range(LOADS):
                        sp.dma_start(x_pair[:, n], xa[0, n]).then_inc(x_in[n], 16)

                    def refill(i, count):
                        for u in range(count):
                            sp.wait_ge(z_done, i * PAIRS + u + 1)
                            sp.wait_ge(bn_done, i * PAIRS + u + 1)
                            v = u + LOADS
                            sp.dma_start(x_pair[:, u % LOADS],
                                         xa[i * 2 + v // GPS, v % GPS]).then_inc(x_in[u % LOADS], 16)

                    if B > 2:
                        with sp.Fori(0, B // 2 - 1) as i:
                            refill(i, PAIRS)
                    refill(B // 2 - 1, PAIRS - LOADS)

                @block.tensor
                def _(pe):
                    pe.wait_ge(const_in, NCONST)

                    def row_modes(i, u):
                        pe.wait_ge(x_in[u % LOADS], i * (16 * PAIRS // LOADS) + 16 * (u // LOADS + 1))
                        for ch in range(2):
                            for j in range(HB):
                                last = nc.tensor.matmul(
                                    z_ps[u % 2][64 * ch:64 * ch + 64], basis_h[:, j],
                                    x_pair[:, u % LOADS, ch, j * W:(j + 1) * W],
                                    start=(j == 0), stop=(j == HB - 1))
                        last.then_inc(z_done, 1)

                    def transpose(i, u):
                        pe.wait_ge(z_copied, i * PAIRS + u + 1)
                        if u >= 2:
                            pe.wait_ge(t_copied, i * PAIRS + u - 1)
                        for k in range(WB):
                            last = nc.tensor.transpose(t_ps[u % 2][:, k], z[:, u % 2, k * P:(k + 1) * P],
                                                       mat[:, IDENT])
                        last.then_inc(t_done, 1)

                    def column_modes(i, s):
                        pe.wait_ge(t_copied, i * PAIRS + GPS * (s + 1))
                        for ki in range(KI):
                            for n in range(2 * WB):
                                k, ri = n // 2, n % 2
                                m = (ki * 2 + ri) * KB
                                last = nc.tensor.matmul(
                                    m_ps[s][:, ki * 2 * M2:(ki + 1) * 2 * M2],
                                    zt[:, s, k, m:m + KB, :], basis_w[:, k, ri],
                                    start=(n == 0), stop=(n == 2 * WB - 1))
                        last.then_inc(m_done, 1)

                    with pe.Fori(0, B // 2) as i:
                        for u in range(PAIRS):
                            row_modes(i, u)
                            if u:
                                transpose(i, u - 1)
                            if u == GPS + 1:
                                column_modes(i, 0)
                        transpose(i, PAIRS - 1)
                        column_modes(i, 1)

                @block.scalar
                def _(act):
                    def copy_z(i, u):
                        act.wait_ge(z_done, i * PAIRS + u + 1)
                        nc.scalar.copy(z[:, u % 2], z_ps[u % 2][:]).then_inc(z_copied, 1)

                    def copy_t(i, u):
                        act.wait_ge(t_done, i * PAIRS + u + 1)
                        g = u % GPS
                        nc.scalar.copy(
                            zt[:, u // GPS, :, :, 2 * g:2 * g + 2].rearrange("p k m c -> p (k m) c"),
                            t_ps[u % 2][:].rearrange("p k (c m) -> p k m c", c=2)).then_inc(t_copied, 1)

                    def copy_m(i, s):
                        act.wait_ge(m_done, i * 2 + s + 1)
                        nc.scalar.copy(modes_x[:, i * 2 + s], m_ps[s][:])

                    with act.Fori(0, B // 2) as i:
                        for u in range(PAIRS):
                            copy_z(i, u)
                            if u:
                                copy_t(i, u - 1)
                            if u == GPS + 2:
                                copy_m(i, 0)
                        copy_t(i, PAIRS - 1)
                        copy_m(i, 1)

                @block.vector
                def _(dve):
                    def aggregate(i, u):
                        dve.wait_ge(bn_done, i * PAIRS + u + 1)
                        dve.sem_inc(agg_begun, 1)
                        for ch in range(2):
                            last = nc.vector.bn_aggr(two_stats[:, u // GPS, 2 * (u % GPS) + ch],
                                                     bn[:, u % 2, ch].rearrange("p j k -> p (j k)"))
                        last.then_inc(bn_agg, 1)

                    with dve.Fori(0, B // 2) as i:
                        for u in range(PAIRS):
                            dve.wait_ge(x_in[u % LOADS], i * (16 * PAIRS // LOADS) + 16 * (u // LOADS + 1))
                            if u >= 2:
                                dve.wait_ge(bn_agg, i * PAIRS + u - 1)
                            for ch in range(2):
                                for j in range(HB):
                                    last = nc.vector.bn_stats(bn[:, u % 2, ch, j],
                                                              x_pair[:, u % LOADS, ch, j * W:(j + 1) * W])
                            last.then_inc(bn_done, 1)
                            if u:
                                aggregate(i, u - 1)
                        aggregate(i, PAIRS - 1)
                        dve.wait_ge(bn_agg, i * PAIRS + PAIRS)
                        nc.vector.tensor_copy(chan_stats[:, ds(i * 2, 2)], two_stats[:]).then_inc(stats_kept, 1)
                        dve.wait_ge(stats_kept, i + 1)

        pm = ExitStack()
        with pm:
            def sb(name, shape, dt=F32):
                return pm.enter_context(nc.sbuf_tensor(name, shape, dt))

            coeff_raw = sb("coeff_raw", [P, 2, 2, M2 * C])
            coeff = sb("coeff", [P, 2, 2, M2, C])
            signed = sb("signed", [P, 2, 2, M2, 2, B])
            ranks = sb("ranks", [P, 2, M2, 2, B])
            proj_in = sb("proj_in", [P, C])
            proj_t = sb("proj_t", [P, C])
            proj_all = sb("proj_all", [P, P])
            squares = sb("squares", [P, B, MODES - 1])
            low_sq = sb("low_sq", [P, B, 2 * KI])
            means = sb("means", [P, B * C])
            gmean = sb("gmean", [P, B, GPS])
            dev = sb("dev", [P, 3, B, C])
            dev4 = sb("dev4", [P, 3, B, KB, C])
            col = sb("col", [P, 3, B])
            vec = sb("vec", [P, 16, B])
            prod = coeff_raw[:].rearrange("p r a j -> p (r a j)")[:, 0:B * MODES].rearrange(
                "p (b m) -> p b m", b=B)
            w_in = sb("w_in", [P, C, TAPS * TAPS])
            w_scaled = sb("w_scaled", [P, TAPS * TAPS, C])
            w_t = sb("w_t", [P, TAPS * TAPS, C])
            w_filter = sb("w_filter", [P, TAPS, FILTER, C])
            w_part = sb("w_part", [P, 2, TAPS, FILTER, C], F16)
            w_max = sb("w_max", [P, 4])
            cols_basis = sb("cols_basis", [P, W])
            rows_basis = sb("rows_basis", [P, H])
            stat_ps = pm.enter_context(nc.psum_tensor("stat_ps", [P, 512], F32))
            r_ps = [pm.enter_context(nc.psum_tensor(f"r_ps{i}", [P, M2, 2, B], F32)) for i in range(2)]
            y_ps = [pm.enter_context(nc.psum_tensor(f"y_ps{i}", [P, M2, 2, B], F32)) for i in range(2)]

            small_in, bases_in, conv_in = sem("small_in"), sem("bases_in"), sem("conv_in")
            coeff_in = [sem(f"coeff_in{i}") for i in range(2)]
            step = sem("step")
            to_pe = sem("to_pe")
            from_pe = sem("from_pe")
            to_act, from_act = sem("to_act"), sem("from_act")
            proj_ready, zeroed = sem("proj_ready"), sem("zeroed")
            turned, signed_ready = sem("turned"), sem("signed_ready")
            ranks_done, ranks_copied = sem("ranks_done"), sem("ranks_copied")
            mix_begun = sem("mix_begun")
            y_real = sem("y_real")
            squared, weights_split = sem("squared"), sem("weights_split")
            y_scaled, y_stored = sem("y_scaled"), sem("y_stored")
            mix_done, y_copied = sem("mix_done"), sem("y_copied")

            CO = 2 * KB * 16
            co = [a.rearrange("r (m k) j c -> k m r (j c)", m=KB) for a in (coeff_re, coeff_im)]
            (FIRST_MEAN, COLS, VAR0, DC, VAR1, BOUND) = range(1, 7)

            with nc.Block() as block:
                @block.sync
                def _(sp):
                    for k in range(KB):
                        sp.dma_start(w_in[k * C:(k + 1) * C], weight.rearrange("o c s t -> o c (s t)")
                                     ).then_inc(conv_in, 16)
                        sp.dma_start(proj_in[k * C:(k + 1) * C], proj).then_inc(small_in, 16)

                    def load_coeff(ki, r):
                        for m in range(KB):
                            for part in range(2):
                                at = (m % 2) * 2 + part
                                sp.dma_start(coeff_raw[at * C:(at + 1) * C, r, m // 2], co[part][ki, m]
                                             ).then_inc(coeff_in[r], 16)

                    load_coeff(0, 0)
                    load_coeff(1, 1)
                    sp.dma_start(cols_basis[:], idft_w).then_inc(bases_in, 16)
                    sp.dma_start(rows_basis[:], idft_h).then_inc(bases_in, 16)
                    with sp.Fori(0, KI // 2 - 1) as i:
                        for r in range(2):
                            sp.wait_ge(turned, i * 2 + r + 1)
                            load_coeff((i + 1) * 2 + r, r)
                    sp.wait_ge(y_scaled, B)
                    sp.dma_start(modes_store, modes_y[:]).then_inc(y_stored, 16)
                    sp.wait_ge(y_stored, 16)

                @block.gpsimd
                def _(pool):
                    for n, t in enumerate((proj_all[:], taps[:], cols_lo[:])):
                        if n:
                            pool.wait_ge(zeroed, n)
                        nc.gpsimd.memset(t, 0.0).then_inc(zeroed, 1)

                @block.tensor
                def _(pe):
                    def small(n, cols, lhs, rhs, start=True, stop=True):
                        return nc.tensor.matmul(stat_ps[:, cols:cols + n], lhs, rhs, start=start, stop=stop)

                    small(B * C, 0, mat[:, MEAN], chan_stats[:, :, :, 0].rearrange("p b c -> p (b c)")
                          ).then_inc(from_pe, 1)
                    pe.wait_ge(to_pe, 1)
                    for k in range(3):
                        for b in range(B):
                            last = small(1, 256 + k * B + b, dev4[:, k, b].rearrange("p m c -> p (m c)"),
                                         mat[:, MEAN, 0:1])
                    last.then_inc(from_pe, 1)
                    pe.wait_ge(to_pe, 2)
                    small(B, 320, mat[:, PAIR], col[:, 1]).then_inc(from_pe, 1)

                    def mix(i, r):
                        pe.wait_ge(turned, i * 2 + r + 1)
                        pe.wait_ge(signed_ready, i * 2 + r + 1)
                        pe.wait_ge(ranks_copied, i * 2 + r + 1)
                        pe.sem_inc(mix_begun, 1)
                        for k2 in range(M2):
                            for m in range(KB):
                                rows = slice((m % 2) * 2 * C, (m % 2 + 1) * 2 * C)
                                last = nc.tensor.matmul(
                                    r_ps[r][m * C:(m + 1) * C, k2].rearrange("p r b -> p (r b)"),
                                    coeff[rows, r, m // 2, k2],
                                    signed[rows, r, m // 2, k2].rearrange("p r b -> p (r b)"),
                                    start=True, stop=True)
                        last.then_inc(ranks_done, 1)

                    def project(i, r):
                        pe.wait_ge(ranks_copied, i * 2 + r + 3)
                        pe.wait_ge(y_copied, i * 2 + r + 1)
                        nc.tensor.matmul(y_ps[r][:].rearrange("p j r b -> p (j r b)"), proj_all[:],
                                         ranks[:, r].rearrange("p j r b -> p (j r b)"),
                                         start=True, stop=True).then_inc(mix_done, 1)

                    pe.wait_ge(proj_ready, 2)
                    with pe.Fori(0, KI // 2) as i:
                        mix(i, 0)
                        mix(i, 1)
                        project(i, 0)
                        project(i, 1)

                    pe.wait_ge(to_pe, 3)
                    small(B, 0, mat[:, DC_DEV], vec[:, 6])
                    small(B, 16, mat[:, DC_PAIR], vec[:, 6]).then_inc(from_pe, 1)
                    pe.wait_ge(to_pe, 4)
                    small(B, 32, mat[:, PAIR_ALL], vec[:, 9], stop=False)
                    small(B, 32, mat[:, PAIR], vec[:, 8], start=False, stop=False)
                    small(B, 32, mat[:, PAIR], col[:, 1], start=False).then_inc(from_pe, 1)
                    pe.wait_ge(to_pe, 5)
                    small(B, 64, mat[:, CHAN], vec[:, 12]).then_inc(from_pe, 1)

                @block.scalar
                def _(act):
                    act.sem_inc(ranks_copied, 2)
                    act.sem_inc(y_copied, 2)
                    act.wait_ge(to_act, 1)
                    nc.scalar.activation(vec[:, 1], vec[:, 0], ACT.Sqrt).then_inc(from_act, 1)

                    def turn(i):
                        for r in range(2):
                            act.wait_ge(ranks_done, i * 2 + r + 3)
                            nc.scalar.copy(ranks[:, r], r_ps[r][:]).then_inc(ranks_copied, 1)
                        for r in range(2):
                            act.wait_ge(mix_done, i * 2 + r + 1)
                            nc.scalar.copy(
                                modes_y[:, :, ds((i * 2 + r) * 2 * M2, 2 * M2)].rearrange(
                                    "p b (r j) -> p j r b", r=2),
                                y_ps[r][:]).then_inc(y_copied, 1)

                    turn(0)
                    act.wait_ge(weights_split, 1)
                    act.wait_ge(zeroed, 3)
                    for first, kb, mb, tap in tap_blocks():
                        for part in range(2):
                            nc.scalar.copy(taps[kb * C:(kb + 1) * C, part, first, :, mb * C:(mb + 1) * C],
                                           w_part[kb * C:(kb + 1) * C, part, tap])
                    with act.Fori(0, KI // 2 - 1) as i:
                        turn(i + 1)

                    act.wait_ge(y_real, 1)
                    for b in range(B):
                        last = nc.scalar.activation(squares[:, b], modes_y[:, b, 1:], ACT.Square,
                                                    accum_out=vec[:, 12, b:b + 1])
                    last.then_inc(squared, 1)

                    for n in range(2):
                        act.wait_ge(to_act, 2 + n)
                        nc.scalar.activation(vec[:, 1], vec[:, 0], ACT.Sqrt).then_inc(from_act, 1)

                @block.vector
                def _(dve):
                    count = [0, 0, 0]

                    def done(ins):
                        count[0] += 1
                        ins.then_inc(step, 1)
                        dve.wait_ge(step, count[0])

                    def tt(o, a, b, op):
                        done(nc.vector.tensor_tensor(o, a, b, op))

                    def ts(o, a, s1, s2, op0, op1=None):
                        if op1 is None:
                            done(nc.vector.tensor_scalar(o, a, s1, None, op0))
                        else:
                            done(nc.vector.tensor_scalar(o, a, s1, s2, op0, op1))

                    def give_pe():
                        count[1] += 1
                        nc.vector.tensor_copy(vec[:, 15, 0:1], vec[:, 15, 1:2]).then_inc(to_pe, 1)

                    def root(v, k):
                        done(nc.vector.tensor_copy(vec[:, 0], v))
                        nc.vector.tensor_copy(vec[:, 15, 0:1], vec[:, 15, 1:2]).then_inc(to_act, 1)
                        dve.wait_ge(from_act, k)
                        done(nc.vector.reciprocal(vec[:, 2], vec[:, 1]))
                        tt(vec[:, 2], vec[:, 2], vec[:, 0], ALU.mult)
                        tt(vec[:, 2], vec[:, 2], vec[:, 1], ALU.add)
                        ts(vec[:, 2], vec[:, 2], 0.5, None, ALU.mult)

                    def phase_c_constants():
                        dve.wait_ge(zeroed, 3)
                        dve.wait_ge(bases_in, 32)
                        done(nc.vector.tensor_copy(cols_hi[:], cols_basis[:]))
                        tt(cols_lo[0:64], cols_basis[0:64], cols_hi[0:64], ALU.subtract)
                        done(nc.vector.tensor_copy(rows_hi[:], rows_basis[:]))
                        tt(rows_basis[:], rows_basis[:], rows_hi[:], ALU.subtract)
                        ts(rows_lo[:], rows_basis[:], mat[:, FIRST_TWO, 0:1], None, ALU.mult)

                        dve.wait_ge(conv_in, 16 * KB)
                        flat = w_in[:].rearrange("p c t -> p (c t)")
                        done(nc.vector.tensor_reduce(w_max[:, 0:1], flat, AX.X, ALU.max))
                        done(nc.vector.tensor_reduce(w_max[:, 1:2], flat, AX.X, ALU.min))
                        ts(w_max[:, 1:2], w_max[:, 1:2], -1.0, TINY, ALU.mult, ALU.max)
                        tt(w_max[:, 0:1], w_max[:, 0:1], w_max[:, 1:2], ALU.max)
                        ts(unscale[:], w_max[:, 0:1], 1.0 / (W_SCALE * G_SCALE), None, ALU.mult)
                        done(nc.vector.reciprocal(w_max[:, 2:3], w_max[:, 0:1]))
                        ts(w_scaled[:], w_in[:].rearrange("p c t -> p t c"), w_max[:, 2:3], W_SCALE, ALU.mult, ALU.mult)
                        done(nc.vector.transpose(w_t[:].rearrange("p t c -> p (t c)"),
                                                 w_scaled[:].rearrange("p t c -> p (t c)")))
                        tap = lambda j: w_t[:].rearrange("p (s t) c -> p s t c", s=TAPS)[:, :, TAPS - 1 - j]
                        for a in range(3):
                            done(nc.vector.tensor_copy(w_filter[:, :, EVEN[0] + a], tap(2 * a)))
                            if a < 2:
                                tt(w_filter[:, :, MID[0] + a], tap(2 * a), tap(2 * a + 1), ALU.add)
                                ts(w_filter[:, :, ODD[0] + a], tap(2 * a + 1), -1.0, None, ALU.mult)
                            else:
                                done(nc.vector.tensor_copy(w_filter[:, :, MID[0] + a], tap(2 * a)))
                        done(nc.vector.tensor_copy(w_part[:, 0], w_filter[:]))
                        nc.vector.tensor_tensor(w_part[:, 1], w_filter[:], w_part[:, 0], ALU.subtract
                                                ).then_inc(weights_split, 1)

                    done(nc.vector.memset(vec[:], 0.0))
                    dve.wait_ge(from_pe, FIRST_MEAN)
                    done(nc.vector.tensor_copy(means[:], stat_ps[:, 0:B * C]))
                    mv = means[:].rearrange("p (b g i) -> p b g i", b=B, i=2)
                    tt(gmean[:], mv[:, :, :, 0], mv[:, :, :, 1], ALU.add)
                    ts(gmean[:], gmean[:], 0.5, None, ALU.mult)
                    gb = gmean[:].rearrange("p b g -> p (b g)").unsqueeze(2).broadcast_to([P, B * GPS, 2])
                    fl = lambda k: dev[:, k].rearrange("p b (g i) -> p (b g) i", i=2)
                    cs = lambda k: chan_stats[:, :, :, k].rearrange("p b (g i) -> p (b g) i", i=2)
                    tt(fl(0), cs(0), gb, ALU.subtract)
                    tt(fl(1), fl(0), fl(0), ALU.mult)
                    tt(fl(1), fl(1), cs(1), ALU.add)
                    done(nc.vector.tensor_copy(fl(2), gb))
                    for m in range(KB):
                        done(nc.vector.tensor_copy(dev4[:, :, :, m].rearrange("p k b c -> p (k b) c"),
                                                   dev[:].rearrange("p k b c -> p (k b) c")))
                    give_pe()

                    dve.wait_ge(small_in, 16 * KB)
                    dve.wait_ge(zeroed, 1)
                    nc.vector.transpose(proj_t[:], proj_in[:]).then_inc(proj_ready, 1)
                    dve.wait_ge(proj_ready, 1)
                    for m in range(KB):
                        at = slice(m * C, (m + 1) * C)
                        last = nc.vector.tensor_copy(proj_all[at, at], proj_t[at])
                    last.then_inc(proj_ready, 1)

                    dve.wait_ge(from_pe, COLS)
                    done(nc.vector.tensor_copy(col[:].rearrange("p k b -> p (k b)"),
                                               stat_ps[:, 256:256 + 3 * B]))
                    give_pe()
                    dve.wait_ge(from_pe, VAR0)
                    ts(vec[:, 3], stat_ps[:, 320:320 + B], GN_EPS, None, ALU.add)
                    root(vec[:, 3], 1)
                    done(nc.vector.reciprocal(vec[:, 4], vec[:, 2]))
                    ts(vec[:, 5], vec[:, 4], -1.0, None, ALU.mult)
                    ts(modes_x[0:C, :, 0], col[0:C, 0], float(HW), None, ALU.mult)

                    dve.sem_inc(ranks_done, 2)
                    def turn(i):
                        for r in range(2):
                            dve.wait_ge(coeff_in[r], i * CO + CO)
                            dve.wait_ge(ranks_done, i * 2 + r + 1)
                            nc.vector.transpose(coeff[:, r].rearrange("p a j c -> p (a j c)"),
                                                coeff_raw[:, r].rearrange("p a j -> p (a j)")
                                                ).then_inc(turned, 1)
                            for m in range(KB):
                                src = slice(m * C, (m + 1) * C)
                                mx = modes_x[src, :, ds((i * 2 + r) * 2 * M2, 2 * M2)].rearrange(
                                    "p b (r j) -> p j r b", r=2)
                                re_at, im_at = [slice(((m % 2) * 2 + part) * C, ((m % 2) * 2 + part + 1) * C)
                                                for part in range(2)]
                                factor = lambda v, n: vec[src, v].unsqueeze(1).unsqueeze(1).broadcast_to(
                                    [C, M2, n, B])
                                nc.vector.tensor_tensor(signed[re_at, r, m // 2], mx, factor(4, 2), ALU.mult)
                                nc.vector.tensor_tensor(signed[im_at, r, m // 2, :, 0:1], mx[:, :, 1:2],
                                                        factor(5, 1), ALU.mult)
                                last = nc.vector.tensor_tensor(signed[im_at, r, m // 2, :, 1:2], mx[:, :, 0:1],
                                                               factor(4, 1), ALU.mult)
                            last.then_inc(signed_ready, 1)

                    turn(0)
                    phase_c_constants()
                    with dve.Fori(0, KI // 2 - 1) as i:
                        turn(i + 1)

                    dve.wait_ge(y_copied, KI + 2)
                    nc.vector.memset(modes_y[0:C, :, M2:M2 + 1], 0.0).then_inc(y_real, 1)
                    dve.wait_ge(y_real, 1)
                    done(nc.vector.tensor_copy(vec[:, 6], modes_y[:, :, 0]))
                    give_pe()
                    tt(prod, modes_y[:], modes_x[:], ALU.mult)
                    done(nc.vector.tensor_reduce(vec[:, 9], prod[:, :, 1:], AX.X, ALU.add))
                    done(nc.vector.tensor_reduce(vec[:, 10], prod[:, :, M2::M2], AX.X, ALU.add))
                    done(nc.vector.scalar_tensor_tensor(vec[:, 9], vec[:, 9], 2.0, vec[:, 10],
                                                        ALU.mult, ALU.subtract))
                    tt(low_sq[:], modes_y[:, :, 0::M2], modes_y[:, :, 0::M2], ALU.mult)
                    done(nc.vector.tensor_reduce(vec[:, 13], low_sq[:, :, 1:], AX.X, ALU.add))
                    dve.wait_ge(squared, 1)
                    done(nc.vector.scalar_tensor_tensor(vec[:, 10], vec[:, 13], -0.75, vec[:, 12],
                                                        ALU.mult, ALU.add))
                    tt(vec[:, 9], vec[:, 9], vec[:, 10], ALU.add)
                    done(nc.vector.scalar_tensor_tensor(vec[:, 13], low_sq[:, :, 0], 0.25, prod[:, :, 0],
                                                        ALU.mult, ALU.add))
                    ts(vec[:, 13], vec[:, 13], mat[:, NO_CONST, 0:1], None, ALU.mult)
                    tt(vec[:, 9], vec[:, 9], vec[:, 13], ALU.add)
                    ts(vec[:, 9], vec[:, 9], 2.0, None, ALU.mult)
                    dve.wait_ge(from_pe, DC)
                    done(nc.vector.tensor_copy(vec[:, 7], stat_ps[:, 0:B]))
                    tt(vec[:, 11], stat_ps[:, 16:16 + B], col[:, 2], ALU.add)
                    done(nc.vector.scalar_tensor_tensor(vec[:, 8], col[:, 0], 2.0, vec[:, 7], ALU.mult, ALU.add))
                    tt(vec[:, 8], vec[:, 8], vec[:, 7], ALU.mult)
                    give_pe()
                    dve.wait_ge(from_pe, VAR1)
                    ts(vec[:, 3], stat_ps[:, 32:32 + B], 0.0, GN_EPS, ALU.max, ALU.add)
                    root(vec[:, 3], 2)
                    done(nc.vector.reciprocal(vec[:, 4], vec[:, 2]))
                    ts(scalars[:, :, GAIN], vec[:, 4], G_SCALE, None, ALU.mult)
                    done(nc.vector.tensor_copy(scalars[:, :, SHIFT], vec[:, 11]))
                    done(nc.vector.scalar_tensor_tensor(modes_y[0:C, :, 0], vec[0:C, 11], -float(HW),
                                                        modes_y[0:C, :, 0], ALU.mult, ALU.add))
                    tt(vec[:, 13], modes_y[:, :, 0], modes_y[:, :, 0], ALU.mult)
                    tt(vec[:, 12], vec[:, 12], vec[:, 13], ALU.add)
                    give_pe()
                    dve.wait_ge(from_pe, BOUND)
                    ts(vec[:, 3], stat_ps[:, 64:64 + B], float(M1), TINY, ALU.mult, ALU.max)
                    root(vec[:, 3], 3)
                    ts(scalars[:, :, ALPHA], vec[:, 2], 1.0 / (Y_SCALE * HW), None, ALU.mult)
                    done(nc.vector.reciprocal(vec[:, 4], vec[:, 2]))
                    ts(scalars[:, :, 3], vec[:, 4], Y_SCALE, None, ALU.mult)
                    for b in range(B):
                        nc.vector.tensor_scalar(modes_y[:, b], modes_y[:, b], scalars[:, b, 3:4], None,
                                                ALU.mult).then_inc(y_scaled, 1)


        before_c.close()
        pc = ExitStack()
        with pc:
            def sb(name, shape, dt=F32):
                return pc.enter_context(nc.sbuf_tensor(name, shape, dt))

            BANKS = 4
            W2 = W // 2
            GH = (W + TAPS - 1) // 2
            EW = W + TAPS
            ROWS = RING * SLOTS
            x_ring = sb("x_ring", [P, ROWS, EW])
            x_edge = sb("x_edge", [P, 1, EW])
            diff = sb("diff", [P, SLOTS, 2, GH])
            e_ring = sb("e_ring", [P, ROWS, 2, GH], F16)
            d_ring = sb("d_ring", [P, ROWS, 2, 2, GH], F16)
            e_edge = sb("e_edge", [P, 1, 2, GH], F16)
            d_edge = sb("d_edge", [P, 1, 2, 2, GH], F16)
            mid = sb("mid", [P, 2, 2, W2])
            o_ring = sb("o_ring", [P, 2, SLOTS, W])
            row_modes = sb("row_modes", [P, 2, Q + 1, KB, C], F16)
            y_modes = sb("y_modes", [P, 2, MODES])
            y_src = sb("y_src", [P, M2, 2, KI, 4], F16)
            y_t = sb("y_t", [P, 2 * M2, C], F16)
            y_one = sb("y_one", [P, BANKS, 2, 2 * M2], F16)
            cur = sb("cur", [P, 2, 4])
            mid_ps, even_ps, odd_ps = [pc.enter_context(nc.psum_tensor(n, [P, 2, W2], F32))
                                       for n in ("mid_ps", "even_ps", "odd_ps")]
            add_ps = pc.enter_context(nc.psum_tensor("add_ps", [P, SLOTS, W], F32))
            row_ps = pc.enter_context(nc.psum_tensor("row_ps", [P, H], F32))
            row_banks = [row_ps[:]] + [t[:].rearrange("p s w -> p (s w)") for t in (mid_ps, even_ps, odd_ps)]

            xl = [sem(f"xl{i}") for i in range(RING)]
            xl_edge = sem("xl_edge")
            cleared = sem("cleared")
            add_done = sem("add_done")
            x1_ready = sem("x1_ready")
            borders = sem("borders")
            diff_ready = sem("diff_ready")
            e_hi, e_lo, d_hi, d_lo = sem("e_hi"), sem("e_lo"), sem("d_hi"), sem("d_lo")
            conv_done = sem("conv_done")
            mid_copied = sem("mid_copied")
            res_top, res_last = sem("res_top"), sem("res_last")
            out_done = sem("out_done")
            stored = [sem(f"stored{i}") for i in range(2)]
            y_in = [sem(f"y_in{i}") for i in range(2)]
            src_ready, one_ready = sem("src_ready"), sem("one_ready")
            rows_done, rows_high, rows_low = sem("rows_done"), sem("rows_high"), sem("rows_low")
            moved, edge_rows = sem("moved"), sem("edge_rows")
            pool_waits = sem("pool_waits")

            ITEMS = NCH + 1
            DIFFS = 2 * NCH + 1
            PPC = SLOTS // 2
            PPS = NCH * PPC
            XB = 64
            CREDIT = 2
            xv = x.rearrange("b c (q m) w -> b m c q w", m=KB)
            ov = out.rearrange("b c (q m) w -> b m c q w", m=KB)
            TURNS = NCH // RING
            SRC = 3
            LEAD = 2

            def blk(m):
                return slice(m * C, (m + 1) * C)

            TOP3, LAST = slice(0, 3 * C), blk(3)

            def middle_channel(n, last):
                if not last:
                    return n
                return {NCH - 4: C - 4, NCH - 3: C - 2}.get(n)

            def end_channel(n, last):
                return {NCH - 4: C - 3, NCH - 3: C - 1}.get(n) if last else None

            def samples(eng, body):
                if B > 2:
                    with eng.Fori(0, B // 2 - 1) as i:
                        body(i * 2, 0, True)
                        body(i * 2 + 1, 1, True)
                body(B - 2, 0, True)
                body(B - 1, 1, False)

            def steps(eng, one):
                with eng.Fori(0, TURNS - 1) as i:
                    for k in range(RING):
                        one(i * RING + k, i, k, False)
                for k in range(RING):
                    one(NCH - RING + k, TURNS - 1, k, True)

            def ahead(b, par, n, k, last, has_next):
                if not last or k < RING - LEAD:
                    return b, par, n + LEAD, (k + LEAD) % RING
                if has_next:
                    return b + 1, 1 - par, k + LEAD - RING, k + LEAD - RING
                return None

            def edge_step(last, k):
                return last and k == RING - LEAD

            def below(ring, edge, k, jp, final):
                at = k * SLOTS + 2 * jp + 1
                if jp < PPC - 1 or (k < RING - 1 and not final):
                    return [(0, 2, ring[:, at:at + 2])]
                return [(0, 1, ring[:, at:at + 1]), (1, 1, edge[:] if final else ring[:, 0:1])]

            with nc.Block() as block:
                @block.sync
                def _(sp):
                    def load(b, n, k):
                        at = slice(k * SLOTS, (k + 1) * SLOTS)
                        for m in range(KB - 1):
                            sp.dma_start(x_ring[blk(m), at, 1:W + 1], xv[b, m, :, ds(n * SLOTS, SLOTS)]
                                         ).then_inc(xl[k], 16)
                        sp.dma_start(x_ring[LAST, at, 1:W + 1], xv[b, 3, :, ds(n * SLOTS - 1, SLOTS)]
                                     ).then_inc(xl[k], 16)

                    def load_first(b):
                        for m in range(KB - 1):
                            sp.dma_start(x_ring[blk(m), 0:SLOTS, 1:W + 1], xv[b, m, :, 0:SLOTS]
                                         ).then_inc(xl[0], 16)
                        sp.dma_start(x_ring[LAST, 0, 1:W + 1], xv[b, 1, :, 0]).then_inc(xl[0], 16)
                        sp.dma_start(x_ring[LAST, 1:SLOTS, 1:W + 1], xv[b, 3, :, 0:SLOTS - 1]
                                     ).then_inc(xl[0], 16)

                    def load_edge(b):
                        for m, (q, r) in enumerate(((Q - 1, 2), (Q - 1, 1), (0, 2), (Q - 1, 3))):
                            sp.dma_start(x_edge[blk(m), 0, 1:W + 1], xv[b, r, :, q]).then_inc(xl_edge, 16)

                    def load_modes(b, par):
                        sp.dma_start(y_modes[:, par], modes_store[:, b]).then_inc(y_in[par], 16)

                    def sample(b, par, has_next):
                        load_edge(b)
                        if not isinstance(b, int) or b < B - 2:
                            sp.wait_ge(src_ready, b * SRC + 2)
                            load_modes(b + 2, par)

                        def one(n, i, k, last):
                            if not last or k == 0:
                                load(b, n + 3, (k + 3) % RING)
                            elif has_next:
                                if k == 1:
                                    load_first(b + 1)
                                else:
                                    load(b + 1, k - 1, k - 1)
                            sp.wait_ge(out_done, (b * NCH + n) * (2 * PPC) + 2 * PPC + CREDIT)
                            for m in range(KB):
                                sp.dma_start(ov[b, m, :, ds(n * SLOTS, SLOTS)], o_ring[blk(m), k % 2]
                                             ).then_inc(stored[k % 2], 16)
                        steps(sp, one)

                    for b in range(2):
                        load_modes(b, b)
                    sp.wait_ge(cleared, 2)
                    load_first(0)
                    load(0, 1, 1)
                    load(0, 2, 2)
                    samples(sp, sample)
                    for r in range(2):
                        sp.wait_ge(stored[r], XB + XB * B * NCH // 2)

                @block.gpsimd
                def _(pool):
                    def border(rows, item):
                        pool.wait_ge(x1_ready, item + 2)
                        pool.sem_inc(pool_waits, 1)
                        nc.gpsimd.tensor_copy(rows[:, :, 0:W + 4:W + 3], rows[:, :, 2:4]).then_inc(borders, 1)
                        nc.gpsimd.tensor_copy(rows[:, :, W + 1:W + 2], rows[:, :, W - 1:W]).then_inc(borders, 1)
                        nc.gpsimd.tensor_copy(rows[:, :, W + 2:W + 3], rows[:, :, W - 2:W - 1]).then_inc(borders, 1)

                    def difference(rows, at, count):
                        nc.gpsimd.tensor_tensor(
                            diff[:, at:at + count].rearrange("p s r w -> p s w r"),
                            rows[:, at:at + count, 0:EW - 1].rearrange("p s (w r) -> p s w r", r=2),
                            rows[:, at:at + count, 1:EW].rearrange("p s (w r) -> p s w r", r=2),
                            ALU.subtract).then_inc(diff_ready, 1)

                    def first_half(b, n, k):
                        rows = x_ring[:, k * SLOTS:(k + 1) * SLOTS]
                        border(rows, b * ITEMS + n)
                        pool.wait_ge(borders, b * (3 * ITEMS) + n * 3 + 3)
                        pool.wait_ge(d_lo, b * ITEMS + n + 1)
                        difference(rows, 0, 2)

                    def second_half(k):
                        difference(x_ring[:, k * SLOTS:(k + 1) * SLOTS], 2, 2)

                    def edge(b):
                        border(x_edge[:], b * ITEMS + NCH)
                        pool.wait_ge(borders, b * (3 * ITEMS) + 3 * ITEMS)
                        pool.wait_ge(d_lo, b * ITEMS + NCH + 1)
                        difference(x_edge[:], 0, 1)

                    def residual(b, n, i, k, jp):
                        pool.wait_ge(mid_copied, b * PPS + n * PPC + jp + 2)
                        if jp == 0:
                            pool.wait_ge(stored[k % 2],
                                         b * (XB * NCH // 2) + i * (XB * RING // 2) + XB * (k // 2) + XB)
                        s = slice(2 * jp, 2 * jp + 2)
                        nc.gpsimd.tensor_tensor(
                            o_ring[TOP3, k % 2, s].rearrange("p s (w r) -> p s w r", r=2),
                            mid[TOP3, jp].unsqueeze(3).broadcast_to([3 * C, 2, W2, 2]),
                            x_ring[TOP3, k * SLOTS + 2 * jp:k * SLOTS + 2 * jp + 2, 1:W + 1].rearrange(
                                "p s (w r) -> p s w r", r=2), ALU.add).then_inc(res_top, 1)

                    def sample(b, par, has_next):
                        def one(n, i, k, last):
                            if edge_step(last, k):
                                edge(b)
                            residual(b, n, i, k, 0)
                            nxt = ahead(b, par, n, k, last, has_next)
                            if nxt:
                                first_half(nxt[0], nxt[2], nxt[3])
                            residual(b, n, i, k, 1)
                            if nxt:
                                second_half(nxt[3])
                        steps(pool, one)

                    nc.gpsimd.memset(x_ring[:, :, EW - 1:EW], 0.0).then_inc(cleared, 1)
                    pool.wait_ge(cleared, 1)
                    nc.gpsimd.memset(x_edge[:, :, EW - 1:EW], 0.0).then_inc(cleared, 1)
                    for n in range(LEAD):
                        first_half(0, n, n)
                        second_half(n)
                    samples(pool, sample)

                @block.tensor
                def _(pe):
                    def add(b, par, n):
                        pe.wait_ge(x1_ready, b * ITEMS + n + 1)
                        if isinstance(n, int) and n == 0:
                            pe.wait_ge(edge_rows, b + 1)
                        for j in range(SLOTS):
                            for basis, first in ((cols_hi, True), (cols_lo, False)):
                                last = nc.tensor.matmul(
                                    add_ps[:, j],
                                    row_modes[:, par].rearrange("p q m c -> p (q m c)")[
                                        :, ds(n * (SLOTS * P) + j * P, P)],
                                    basis[:], start=first, stop=not first)
                        last.then_inc(add_done, 1)

                    def add_edge(b, par):
                        pe.wait_ge(x1_ready, b * ITEMS + NCH + 1)
                        for basis, first in ((cols_hi, True), (cols_lo, False)):
                            last = nc.tensor.matmul(
                                add_ps[:, 0], row_modes[:, par, Q].rearrange("p m c -> p (m c)"),
                                basis[:], start=first, stop=not first)
                        last.then_inc(add_done, 1)

                    def rows(b, o, place=0, bank=0, banks=1):
                        pe.wait_ge(one_ready, b * C + o + 1)
                        pe.wait_ge(rows_low, b * C + o + 1 + BANKS - banks)
                        lhs = y_one[:, place].rearrange("p d m -> p (d m)")
                        nc.tensor.matmul(row_banks[bank], lhs, rows_hi[:], start=True, stop=False)
                        nc.tensor.matmul(row_banks[bank], lhs, rows_lo[:], start=False, stop=True
                                         ).then_inc(rows_done, 1)

                    def product(ps, filt, ring, edge, pick, k, jp, final):
                        first_tap, length = filt
                        at = k * SLOTS + 2 * jp
                        todo = []
                        for group, pieces in ((0, [(0, 2, ring[:, at:at + 2])]),
                                              (1, below(ring, edge, k, jp, final))):
                            for a in range(length):
                                for w_part, g_part in ((0, 0), (0, 1), (1, 0)):
                                    for row, count, data in pieces:
                                        todo.append((ps[:, row:row + count],
                                                     taps[:, w_part, group, first_tap + a],
                                                     pick(data, g_part)[:, :, a:a + W2]))
                        for e, (o, lhs, rhs) in enumerate(todo):
                            last = nc.tensor.matmul(o, lhs, rhs, start=(e == 0), stop=(e == len(todo) - 1),
                                                    skip_group_check=True)
                        last.then_inc(conv_done, 1)

                    def conv(b, n, k, jp, final):
                        item = b * ITEMS + n + jp // (PPC - 1)
                        pe.wait_ge(e_lo, item + 1)
                        pe.wait_ge(mid_copied, b * PPS + n * PPC + jp + 1)
                        product(mid_ps, MID, e_ring, e_edge, lambda d, p: d[:, :, p], k, jp, final)
                        pe.wait_ge(d_lo, item + 2)
                        pe.wait_ge(out_done, b * (2 * PPS) + n * (2 * PPC) + 2 * jp + 1)
                        product(even_ps, EVEN, d_ring, d_edge, lambda d, p: d[:, :, 0, p], k, jp, final)
                        pe.wait_ge(out_done, b * (2 * PPS) + n * (2 * PPC) + 2 * jp + 2)
                        product(odd_ps, ODD, d_ring, d_edge, lambda d, p: d[:, :, 1, p], k, jp, final)

                    def sample(b, par, has_next):
                        def one(n, i, k, last):
                            final = last and k == RING - 1
                            if edge_step(last, k):
                                add_edge(b, par)
                            conv(b, n, k, 0, False)
                            nxt = ahead(b, par, n, k, last, has_next)
                            if nxt:
                                add(*nxt[:3])
                            if has_next and middle_channel(n, last) is not None:
                                rows(b + 1, middle_channel(n, last))
                            conv(b, n, k, 1, final)
                            if has_next and end_channel(n, last):
                                rows(b + 1, end_channel(n, last), 1)
                        steps(pe, one)

                    with pe.Fori(0, C // BANKS) as i:
                        for u in range(BANKS):
                            rows(0, i * BANKS + u, u, u, BANKS)
                    for n in range(LEAD):
                        add(0, 0, n)
                    samples(pe, sample)

                @block.scalar
                def _(act):
                    def rows(b, par, o, bank=0):
                        act.wait_ge(rows_done, b * C + o + 1)
                        nc.scalar.copy(
                            row_modes[:, par, 0:Q, :, ds(o, 1)].rearrange("p q m c -> p (q m c)"),
                            row_banks[bank]).then_inc(rows_high, 1)

                    def high(out_, in_, par, ready):
                        nc.scalar.activation(out_, in_, ACT.Copy, scale=cur[:, par, GAIN:GAIN + 1]
                                             ).then_inc(ready, 1)

                    def high_e(b, par, n, k):
                        s = slice(k * SLOTS, (k + 1) * SLOTS)
                        act.wait_ge(borders, b * (3 * ITEMS) + n * 3 + 3)
                        high(e_ring[:, s, 0], x_ring[:, s, 1:EW:2], par, e_hi)

                    def high_d(b, par, n, k):
                        s = slice(k * SLOTS, (k + 1) * SLOTS)
                        act.wait_ge(diff_ready, b * DIFFS + n * 2 + 2)
                        high(d_ring[:, s, :, 0].rearrange("p s r w -> p (s r) w"),
                             diff[:].rearrange("p s r w -> p (s r) w"), par, d_hi)

                    def high_edge(b, par):
                        act.wait_ge(borders, b * (3 * ITEMS) + 3 * ITEMS)
                        high(e_edge[:, :, 0], x_edge[:, :, 1:EW:2], par, e_hi)
                        act.wait_ge(diff_ready, b * DIFFS + DIFFS)
                        high(d_edge[:, 0, :, 0], diff[:, 0], par, d_hi)

                    def copy_mid(b, par, n, jp):
                        act.wait_ge(conv_done, b * (3 * PPS) + n * (3 * PPC) + 3 * jp + 1)
                        nc.scalar.activation(mid[:, jp], mid_ps[:], ACT.Identity, scale=unscale[:],
                                             bias=cur[:, par, SHIFT:SHIFT + 1]).then_inc(mid_copied, 1)

                    def sample(b, par, has_next):
                        def one(n, i, k, last):
                            if edge_step(last, k):
                                high_edge(b, par)
                            copy_mid(b, par, n, 0)
                            nxt = ahead(b, par, n, k, last, has_next)
                            if nxt:
                                high_e(*nxt)
                            if has_next and middle_channel(n, last) is not None:
                                rows(b + 1, 1 - par, middle_channel(n, last))
                            copy_mid(b, par, n, 1)
                            if nxt:
                                high_d(*nxt)
                            if has_next and end_channel(n, last):
                                rows(b + 1, 1 - par, end_channel(n, last))
                        steps(act, one)

                    act.sem_inc(mid_copied, 1)
                    with act.Fori(0, C // BANKS) as i:
                        for u in range(BANKS):
                            rows(0, 0, i * BANKS + u, u)
                    for n in range(LEAD):
                        high_e(0, 0, n, n)
                        high_d(0, 0, n, n)
                    samples(act, sample)

                @block.vector
                def _(dve):
                    def source(b, par):
                        nc.vector.tensor_copy(cur[:, par], scalars[:, b])
                        dve.wait_ge(y_in[par], (b - par) * 8 + 16)
                        my = y_modes[:, par].rearrange("p (k r j) -> p j k r", k=KI, r=2)
                        plan = ((0, 0, 0, 1.0), (0, 1, 1, -1.0), (1, 0, 1, 1.0), (1, 1, 0, 1.0))
                        for t, s, r, sign in plan:
                            last = nc.vector.tensor_scalar(y_src[:, :, t, :, s], my[:, :, :, r], sign, None, ALU.mult)
                        last.then_inc(src_ready, 1)
                        dve.wait_ge(src_ready, b * SRC + 1)
                        for t, s, r, sign in plan:
                            last = nc.vector.scalar_tensor_tensor(
                                y_src[:, :, t, :, 2 + s], my[:, :, :, r], sign, y_src[:, :, t, :, s],
                                ALU.mult, ALU.subtract)
                        last.then_inc(src_ready, 1)
                        dve.wait_ge(src_ready, b * SRC + 2)
                        nc.vector.transpose(y_t[:].rearrange("p m c -> p (m c)"),
                                            y_src[:].rearrange("p j t k s -> p (j t k s)")).then_inc(src_ready, 1)

                    def one_channel(b, o, place=0):
                        dve.wait_ge(src_ready, b * SRC + SRC)
                        nc.vector.tensor_copy(
                            y_one[:, place], y_t[:, :, ds(o, 1)].rearrange("p m c -> p c m").broadcast_to([P, 2, 2 * M2])
                        ).then_inc(one_ready, 1)

                    def low_rows(b, par, o, bank=0):
                        dve.wait_ge(rows_high, b * C + o + 1)
                        lo = slice(64, P)
                        ap = row_modes[lo, par, 0:Q, :, ds(o, 1)].rearrange("p q m c -> p (q m c)")
                        nc.vector.tensor_tensor(ap, row_banks[bank][lo], ap, ALU.subtract).then_inc(rows_low, 1)

                    def move_edge_rows(b, par):
                        dve.wait_ge(rows_low, b * C + C + BANKS)
                        rm = row_modes[:, par]
                        nc.vector.tensor_copy(rm[:, Q, 0], rm[:, Q - 1, 2])
                        nc.vector.tensor_copy(rm[:, Q, 1], rm[:, Q - 1, 1])
                        nc.vector.tensor_copy(rm[:, Q, 2], rm[:, 0, 2])
                        nc.vector.tensor_copy(rm[:, Q, 3], rm[:, 0, 3]).then_inc(moved, 1)
                        dve.wait_ge(moved, b + 1)
                        nc.vector.tensor_copy(rm[:, 0, 3], rm[:, 0, 1]).then_inc(edge_rows, 1)

                    def loaded(b, n, k):
                        per = XB * TURNS
                        if k == 0:
                            dve.wait_ge(xl[0], b * (per + 16) + n * (XB // RING) + XB + 16)
                        else:
                            dve.wait_ge(xl[k], b * per + (n - k) * (XB // RING) + XB)

                    def add(b, par, n, k):
                        loaded(b, n, k)
                        dve.wait_ge(add_done, b * ITEMS + n + 1)
                        rows = x_ring[:, k * SLOTS:(k + 1) * SLOTS, 1:W + 1]
                        nc.vector.scalar_tensor_tensor(rows, add_ps[:], cur[:, par, ALPHA:ALPHA + 1], rows,
                                                       ALU.mult, ALU.add).then_inc(x1_ready, 1)

                    def add_edge(b, par):
                        dve.wait_ge(xl_edge, b * 64 + 64)
                        dve.wait_ge(add_done, b * ITEMS + ITEMS)
                        rows = x_edge[:, 0, 1:W + 1]
                        nc.vector.scalar_tensor_tensor(rows, add_ps[:, 0], cur[:, par, ALPHA:ALPHA + 1], rows,
                                                       ALU.mult, ALU.add).then_inc(x1_ready, 1)

                    def low(out_, in_, high, par, ready):
                        nc.vector.scalar_tensor_tensor(out_, in_, cur[:, par, GAIN:GAIN + 1], high,
                                                       ALU.mult, ALU.subtract).then_inc(ready, 1)

                    def low_e(b, par, n, k):
                        s = slice(k * SLOTS, (k + 1) * SLOTS)
                        dve.wait_ge(e_hi, b * ITEMS + n + 1)
                        low(e_ring[:, s, 1], x_ring[:, s, 1:EW:2], e_ring[:, s, 0], par, e_lo)

                    def low_d(b, par, n, k):
                        d = d_ring[:, k * SLOTS:(k + 1) * SLOTS].rearrange("p s r h w -> p (s r) h w")
                        dve.wait_ge(d_hi, b * ITEMS + n + 1)
                        low(d[:, :, 1], diff[:].rearrange("p s r w -> p (s r) w"), d[:, :, 0], par, d_lo)

                    def low_edge(b, par):
                        dve.wait_ge(e_hi, b * ITEMS + ITEMS)
                        low(e_edge[:, 0, 1], x_edge[:, 0, 1:EW:2], e_edge[:, 0, 0], par, e_lo)
                        dve.wait_ge(d_hi, b * ITEMS + ITEMS)
                        low(d_edge[:, 0, :, 1], diff[:, 0], d_edge[:, 0, :, 0], par, d_lo)

                    def residual(b, n, i, k, jp, final):
                        dve.wait_ge(mid_copied, b * PPS + n * PPC + jp + 2)
                        if jp == 0:
                            dve.wait_ge(stored[k % 2],
                                        b * (XB * NCH // 2) + i * (XB * RING // 2) + XB * (k // 2) + XB)
                        for row, count, data in below(x_ring, x_edge, k, jp, final):
                            last = nc.vector.tensor_tensor(
                                o_ring[LAST, k % 2, 2 * jp + row:2 * jp + row + count].rearrange(
                                    "p s (w r) -> p s w r", r=2),
                                mid[LAST, jp, row:row + count].unsqueeze(3).broadcast_to([C, count, W2, 2]),
                                data[LAST, :, 1:W + 1].rearrange("p s (w r) -> p s w r", r=2), ALU.add)
                        last.then_inc(res_last, 1)

                    def finish(b, n, k, jp, odd):
                        dve.wait_ge(conv_done, b * (3 * PPS) + n * (3 * PPC) + 3 * jp + 2 + odd)
                        if not odd:
                            dve.wait_ge(res_top, b * PPS + n * PPC + jp + 1)
                            dve.wait_ge(res_last, b * PPS + n * PPC + jp + 1)
                        o = o_ring[:, k % 2, 2 * jp:2 * jp + 2, odd::2]
                        nc.vector.scalar_tensor_tensor(o, (odd_ps if odd else even_ps)[:], unscale[:], o,
                                                       ALU.mult, ALU.add).then_inc(out_done, 1)

                    def sample(b, par, has_next):
                        if has_next:
                            source(b + 1, 1 - par)

                        def one(n, i, k, last):
                            final = last and k == RING - 1
                            if edge_step(last, k):
                                add_edge(b, par)
                                low_edge(b, par)
                            if has_next and middle_channel(n, last) is not None:
                                one_channel(b + 1, middle_channel(n, last))
                            if has_next and end_channel(n, last):
                                one_channel(b + 1, end_channel(n, last), 1)
                            residual(b, n, i, k, 0, False)
                            finish(b, n, k, 0, 0)
                            finish(b, n, k, 0, 1)
                            nxt = ahead(b, par, n, k, last, has_next)
                            if nxt:
                                add(*nxt)
                            if has_next and middle_channel(n, last) is not None:
                                low_rows(b + 1, 1 - par, middle_channel(n, last))
                            if nxt:
                                low_e(*nxt)
                            residual(b, n, i, k, 1, final)
                            finish(b, n, k, 1, 0)
                            if nxt:
                                low_d(*nxt)
                            finish(b, n, k, 1, 1)
                            if has_next and end_channel(n, last):
                                low_rows(b + 1, 1 - par, end_channel(n, last))
                                if end_channel(n, last) == C - 1:
                                    move_edge_rows(b + 1, 1 - par)
                        steps(dve, one)

                    dve.sem_inc(rows_low, BANKS)
                    dve.sem_inc(x1_ready, 1)
                    dve.sem_inc(d_lo, 1)
                    dve.sem_inc(out_done, CREDIT)
                    for r in range(2):
                        dve.sem_inc(stored[r], XB)
                    source(0, 0)
                    for u in range(BANKS):
                        one_channel(0, u, u)
                    with dve.Fori(0, C // BANKS - 1) as i:
                        for u in range(BANKS):
                            low_rows(0, 0, i * BANKS + u, u)
                            one_channel(0, i * BANKS + BANKS + u, u)
                    for u in range(BANKS):
                        low_rows(0, 0, C - BANKS + u, u)
                    move_edge_rows(0, 0)
                    dve.wait_ge(cleared, 2)
                    for n in range(LEAD):
                        add(0, 0, n, n)
                        low_e(0, 0, n, n)
                        low_d(0, 0, n, n)
                    samples(dve, sample)


def tap_blocks():
    found = []
    for first in range(2):
        for kb in range(KB):
            row_in = KB * first + (kb if kb < 3 else -1)
            for mb in range(KB):
                s = mb + 3 - row_in
                if 0 <= s < TAPS:
                    found.append((first, kb, mb, s))
    assert len(found) == KB * TAPS
    return found


def kernel(x, L0_conv_coeff_real, L0_conv_coeff_imag, L0_conv_proj, L1_conv_weight):
    import concourse.bacc as bacc
    from concourse.bass_utils import run_bass_kernel_spmd

    nc = bacc.Bacc("TRN2", target_bir_lowering=False, num_devices=1)
    data = dict(x=x, coeff_re=L0_conv_coeff_real, coeff_im=L0_conv_coeff_imag, proj=L0_conv_proj,
                weight=L1_conv_weight)
    arrays = {n: np.ascontiguousarray(a) for n, a in data.items()}
    arrays.update(constant_tables(*arrays["x"].shape[2:]))
    args = [nc.dram_tensor(n, list(a.shape), F32, kind="ExternalInput").ap() for n, a in arrays.items()]
    args.append(nc.dram_tensor("result", list(arrays["x"].shape), F32, kind="ExternalOutput").ap())
    two_conv_layers(nc, *args)
    return run_bass_kernel_spmd(nc, [arrays], core_ids=[0]).results[0]["result"]
```
